# Optimizing a Trainium2 kernel written in Bass

```python
import numpy as np
import jax
import jax.numpy as jnp

def _softmax(x, axis=-1):
    return jax.nn.softmax(x, axis=axis)

def _gelu(x):
    return jax.nn.gelu(x, approximate=True)

def _silu(x):
    return jax.nn.silu(x)

def _sigmoid(x):
    return jax.nn.sigmoid(x)

def _layernorm(x, axis=-1, eps=1e-05):
    m = jnp.mean(x, axis=axis, keepdims=True)
    v = jnp.var(x, axis=axis, keepdims=True)
    return (x - m) / jnp.sqrt(v + eps)

def _scatter_add(tgt, idx, src, axis=0):
    return tgt.at[idx].add(src)

def _segment_sum(src, seg, n):
    return jax.ops.segment_sum(src, seg, n)
kernel_name = 'mk_gnn_preln_d2_gnn_r8_15b216'

def setup_inputs(seed: int=0):
    np.random.seed(seed)
    _w = jnp.asarray

    def _rec_inputs():
        import jax
        import jax.numpy as jnp
        _gk = jax.random.key(seed)
        x = -0.000202 + 1 * jax.random.normal(jax.random.fold_in(_gk, 1), (12500, 128), jnp.float32)
        src = jax.random.randint(jax.random.fold_in(_gk, 2), (400000,), 0, 12500, jnp.int32)
        dst = jax.random.randint(jax.random.fold_in(_gk, 3), (400000,), 0, 12500, jnp.int32)
        _o = jnp.argsort(dst, stable=True)
        src = src[_o]
        dst = dst[_o]
        edge_attr_64 = -7.08334e-05 + 0.999895 * jax.random.normal(jax.random.fold_in(_gk, 12), (400000, 64), jnp.float32)
        edge_type_8 = jax.random.randint(jax.random.fold_in(_gk, 14), (400000,), 0, 8, jnp.int32)
        edge_weight1 = jax.random.uniform(jax.random.fold_in(_gk, 15), (400000, 1), jnp.float32, 0.0, 0.999998)
        return (x, src, dst, edge_attr_64, edge_type_8, edge_weight1)
    x, src, dst, edge_attr_64, edge_type_8, edge_weight1 = _rec_inputs()

    def _L0_gnn_setup():
        import jax, jax.numpy as jnp
        import numpy as np
        N, E = (6250, 75000)
        NODE_DIM, EDGE_DIM, MSG_DIM = (128, 64, 128)
        key = jax.random.key(seed)
        ks = jax.random.split(key, 8)
        s = 0.05
        return {'node_features': jax.random.normal(ks[0], (N, NODE_DIM), jnp.float32), 'edge_features': jax.random.normal(ks[1], (E, EDGE_DIM), jnp.float32), 'edge_index': jax.random.randint(ks[2], (2, E), 0, N, jnp.int32), 'We1': jax.random.normal(ks[3], (2 * NODE_DIM + EDGE_DIM, 32), jnp.float32) * s, 'be1': jnp.zeros((32,), jnp.float32), 'We2': jax.random.normal(ks[4], (32, MSG_DIM), jnp.float32) * s, 'be2': jnp.zeros((MSG_DIM,), jnp.float32), 'Wn1': jax.random.normal(ks[5], (NODE_DIM + MSG_DIM, 64), jnp.float32) * s, 'bn1': jnp.zeros((64,), jnp.float32), 'Wn2': jax.random.normal(ks[6], (64, MSG_DIM), jnp.float32) * s, 'bn2': jnp.zeros((MSG_DIM,), jnp.float32)}
    _L0_gnn_all = _L0_gnn_setup()
    _L0_gnn_in = {k: v for k, v in _L0_gnn_all.items() if k in ('We1', 'be1', 'We2', 'be2', 'Wn1', 'bn1', 'Wn2', 'bn2')}
    del _L0_gnn_all

    def _L1_gnn_setup():
        import jax, jax.numpy as jnp
        import numpy as np
        N_NODES = 6250
        N_EDGES = 200000
        IN_FEAT = 128
        OUT_FEAT = 128
        NUM_RELS = 8
        key = jax.random.key(seed)
        k_h, k_src, k_dst, k_et, k_nrm, k_w, k_b = jax.random.split(key, 7)
        h = jax.random.normal(k_h, (N_NODES, IN_FEAT), dtype=jnp.float32)
        src = jax.random.randint(k_src, (N_EDGES,), 0, N_NODES, dtype=jnp.int32)
        dst = jax.random.randint(k_dst, (N_EDGES,), 0, N_NODES, dtype=jnp.int32)
        etype = jax.random.randint(k_et, (N_EDGES,), 0, NUM_RELS, dtype=jnp.int32)
        norm = jax.random.uniform(k_nrm, (N_EDGES, 1), dtype=jnp.float32)
        W = jax.random.normal(k_w, (NUM_RELS, IN_FEAT, OUT_FEAT), dtype=jnp.float32)
        b = jax.random.normal(k_b, (NUM_RELS, OUT_FEAT), dtype=jnp.float32)
        return {'h': h, 'src': src, 'dst': dst, 'etype': etype, 'norm': norm, 'W': W, 'b': b}
    _L1_gnn_all = _L1_gnn_setup()
    _L1_gnn_in = {k: v for k, v in _L1_gnn_all.items() if k in ('W', 'b')}
    del _L1_gnn_all
    return {'x': x, 'src': src, 'dst': dst, 'edge_attr_64': edge_attr_64, 'edge_type_8': edge_type_8, 'edge_weight1': edge_weight1, 'L0_gnn_We1': _L0_gnn_in['We1'], 'L0_gnn_be1': _L0_gnn_in['be1'], 'L0_gnn_We2': _L0_gnn_in['We2'], 'L0_gnn_be2': _L0_gnn_in['be2'], 'L0_gnn_Wn1': _L0_gnn_in['Wn1'], 'L0_gnn_bn1': _L0_gnn_in['bn1'], 'L0_gnn_Wn2': _L0_gnn_in['Wn2'], 'L0_gnn_bn2': _L0_gnn_in['bn2'], 'L1_gnn_W': _L1_gnn_in['W'], 'L1_gnn_b': _L1_gnn_in['b']}

def reference(x, src, dst, edge_attr_64, edge_type_8, edge_weight1, L0_gnn_We1, L0_gnn_be1, L0_gnn_We2, L0_gnn_be2, L0_gnn_Wn1, L0_gnn_bn1, L0_gnn_Wn2, L0_gnn_bn2, L1_gnn_W, L1_gnn_b):
    import jax
    import jax.numpy as jnp

    def _L0_gnn_ref(node_features, edge_features, edge_index, We1, be1, We2, be2, Wn1, bn1, Wn2, bn2):
        import jax, jax.numpy as jnp
        import numpy as np
        N, E = (6250, 75000)
        NODE_DIM, EDGE_DIM, MSG_DIM = (128, 64, 128)
        src, dst = (edge_index[0], edge_index[1])
        src_f = node_features[src]
        dst_f = node_features[dst]
        edge_in = jnp.concatenate([src_f, dst_f, edge_features], axis=1)
        h = jax.nn.relu(edge_in @ We1 + be1)
        edge_msg = jax.nn.relu(h @ We2 + be2)
        node_in = jnp.concatenate([dst_f, edge_msg], axis=1)
        h2 = jax.nn.relu(node_in @ Wn1 + bn1)
        node_msg = jax.nn.relu(h2 @ Wn2 + bn2)
        agg = jax.ops.segment_sum(node_msg, dst, num_segments=node_features.shape[0])
        return node_features + agg

    def _L1_gnn_ref(h, src, dst, etype, norm, W, b):
        import jax, jax.numpy as jnp
        import numpy as np
        N_NODES = 6250
        N_EDGES = 200000
        IN_FEAT = 128
        OUT_FEAT = 128
        NUM_RELS = 8
        H = jnp.einsum('ni,rio->rno', h, W)
        msg = (H[etype, src] + b[etype]) * norm
        out = jax.ops.segment_sum(msg, dst, num_segments=h.shape[0])
        return jax.nn.relu(out)
    edge_index = jnp.stack([src, dst])
    h = jnp.maximum(_layernorm(x, axis=-1), 0.0)
    x = x + _L0_gnn_ref(h, edge_attr_64, edge_index, L0_gnn_We1, L0_gnn_be1, L0_gnn_We2, L0_gnn_be2, L0_gnn_Wn1, L0_gnn_bn1, L0_gnn_Wn2, L0_gnn_bn2)
    h = jnp.maximum(_layernorm(x, axis=-1), 0.0)
    x = x + _L1_gnn_ref(h, src, dst, edge_type_8, edge_weight1, L1_gnn_W, L1_gnn_b)
    return x

_drawn_inputs = setup_inputs


def setup_inputs(seed=0):
    import zlib

    import numpy as np

    out = dict(_drawn_inputs(seed))
    spreads = {'L0_gnn_be1': (0.0, 0.8),
     'L0_gnn_be2': (0.0, 0.1),
     'L0_gnn_bn1': (0.0, 0.1),
     'L0_gnn_bn2': (0.0, 0.1)}
    factors = {'edge_attr_64': 8.0}
    for name, (base, spread) in spreads.items():
        noise = np.random.default_rng([zlib.crc32(name.encode()), seed]).standard_normal(out[name].shape)
        drawn = base * np.exp(spread * noise) if base else spread * noise
        out[name] = jnp.asarray(drawn.astype(out[name].dtype))
    for name, factor in factors.items():
        out[name] = (out[name] * factor).astype(out[name].dtype)
    return out
```

```python
import concourse.bass as bass
from concourse import mybir
from contextlib import ExitStack


def gnn_two_layers(nc, x, src_t, dst_t, etype_t, weight_t, dst_c, edge_attr,
                   we1, be1, we2, be2, wn1, bn1, wn2, bn2, w_rel, b_rel, out):
    f32, bf16, i32, u32 = mybir.dt.float32, mybir.dt.bfloat16, mybir.dt.int32, mybir.dt.uint32
    ALU, ACT, AX = mybir.AluOpType, mybir.ActivationFunctionType, mybir.AxisListType
    ds = bass.ds

    P = 128
    NPAD, D = x.shape
    TPG = 7
    NG = NPAD // (P * TPG)
    NTILE = NG * TPG
    TC = 4
    CH = TC * P
    NCH = dst_c.shape[0]
    SL = 4
    W = 32
    EA = edge_attr.shape[1]
    H1 = we2.shape[0]
    H2 = wn2.shape[0]
    QR = H1 + H2
    R = w_rel.shape[0]
    MAXPASS = (NPAD + W - 1) // W
    TOP = NPAD - W
    EPS = 1e-5
    assert NG % 2 == 0 and NCH % SL == 0 and TC * H1 == P and 2 * H2 == P and 2 * EA == P and 3 * W <= P
    QP = max(q for q in range(1, P + 1) if NCH % q == 0)
    QC = NCH // QP

    p_tab = nc.dram_tensor("p_tab", [NPAD, H1], f32).ap()
    qr_tab = [nc.dram_tensor(f"qr_tab{k}", [NPAD, QR], bf16).ap() for k in range(3)]
    rel_tab = nc.dram_tensor("rel_tab", [NPAD * R, D], f32).ap()
    row_tab = nc.dram_tensor("row_tab", [P, NCH * TC], i32).ap()
    base_d = nc.dram_tensor("base_d", [QP, QC], f32).ap()
    range_d = nc.dram_tensor("range_d", [QP, QC], f32).ap()

    ctx = ExitStack()
    with ctx:
        def sb(name, shape, dt=f32):
            return ctx.enter_context(nc.sbuf_tensor(name, shape, dt))

        def sem(name):
            return ctx.enter_context(nc.semaphore(name))

        def slot_sems(name, n=SL):
            return [sem(f"{name}{k}") for k in range(n)]

        w_node = sb("w_node", [P, P])
        bias_node = sb("bias_node", [P, P])
        w1_pair = sb("w1_pair", [P, 2, P])
        w2_tile = sb("w2_tile", [P, TC, P])
        wn1_msg = sb("wn1_msg", [P, H2])
        wn2_half = sb("wn2_half", [P, 2, P])
        be2_col = sb("be2_col", [P, 1])
        bn2_rows = sb("bn2_rows", [3 * W, TC * D], bf16)
        ones_b = sb("ones_b", [3 * W, P], bf16)
        w_rel_sb = sb("w_rel_sb", [P, R, D])
        b_rel_sb = sb("b_rel_sb", [P, R * D])
        ident = sb("ident", [P, P])
        ident_b = sb("ident_b", [P, P], bf16)
        iota_i = sb("iota_i", [P, 3 * W], i32)
        iota_f = sb("iota_f", [P, 3 * W])

        dst_f = sb("dst_f", [P, NCH * TC])
        rel_f = sb("rel_f", [P, NCH * TC])
        w_f = sb("w_f", [P, NCH * TC])
        least = sb("least", [QP, QC])
        most = sb("most", [QP, QC])
        base0 = sb("base0", [P, NCH])
        base_f = sb("base_f", [P, NCH])
        base_i = sb("base_i", [P, NCH], i32)
        range_max = sb("range_max", [1, 1])
        passes_f = sb("passes_f", [1, 1])
        passes_i = sb("passes_i", [1, 1], i32)

        res = sb("res", [P, NTILE, D])
        agg = sb("agg", [P, NPAD])
        taken = 0

        def in_agg(n, parts=P):
            nonlocal taken
            taken += n
            assert taken <= NPAD
            return agg[0:parts, taken - n:taken]

        dst_rows = in_agg(QC * CH, QP).bitcast(i32).rearrange("q (k e) -> q k e", e=CH)
        etype_i = in_agg(NCH * TC).bitcast(i32)
        range_row = in_agg(NCH, 1)
        pass_i = in_agg(MAXPASS, 1).bitcast(i32)
        pass_f = in_agg(MAXPASS, 1)
        bn2_rep = in_agg(TC * D, 3 * W)
        bn2_res = in_agg(TC * D, 3 * W)
        bn2_part = in_agg(TC * D // 2, 3 * W).bitcast(bf16)
        x_in = sb("x_in", [P, 2, TPG, D])
        h = sb("h", [P, TPG, D])
        hT = sb("hT", [P, TPG * P])
        stats = sb("stats", [P, TPG, 6])
        mv = sb("mv", [P, TPG, 2])
        var_eps = sb("var_eps", [P, TPG])
        std = sb("std", [P, TPG])
        rstd = sb("rstd", [P, TPG])
        agg_group = sb("agg_group", [P, TPG * P])
        shared = sb("shared", [P, max(TPG * (P + QR) + 3 * TPG * QR // 2, SL * TC * (EA + H1) + 2 * CH)])
        taken_by = {"tables": 0, "edges": 0}

        def in_shared(who, n):
            taken_by[who] += n
            return shared[:, taken_by[who] - n:taken_by[who]]

        pqr = in_shared("tables", TPG * P).rearrange("p (j d) -> p j d", d=P)
        qr_res = in_shared("tables", TPG * QR).rearrange("p (j d) -> p j d", d=QR)
        qr_hi, qr_mid, qr_lo = (in_shared("tables", TPG * QR // 2).bitcast(bf16).rearrange("p (j d) -> p j d", d=QR)
                                for _ in range(3))
        ea = [in_shared("edges", TC * EA) for s in range(SL)]
        prow = [in_shared("edges", TC * H1).rearrange("p (t o) -> p t o", o=H1) for s in range(SL)]
        msg1_sb, msg2_sb = (in_shared("edges", CH) for _ in range(2))
        rel_place = sb("rel_place", [P, max(2 * R * D, SL * TC * D)])
        rel_rows = rel_place[:, 0:2 * R * D].rearrange("p (b n) -> p b n", b=2)
        rows = [rel_place[:, s * TC * D:(s + 1) * TC * D].rearrange("p (t d) -> p t d", d=D) for s in range(SL)]

        idx = [sb(f"idx{s}", [P, TC], i32) for s in range(SL)]
        qr_w = [sb(f"qr_w{s}", [3 * W, QR], bf16) for s in range(SL)]
        hot = [sb(f"hot{s}", [P, TC, W]) for s in range(SL)]
        hot3 = [sb(f"hot3{s}", [P, TC, 3 * W], bf16) for s in range(SL)]
        eaT = sb("eaT", [P, 2 * P])
        hotT = [sb(f"hotT{s}", [3 * W, CH], bf16) for s in range(2)]
        h1_sb = sb("h1_sb", [P, P])
        h2_sb = sb("h2_sb", [P, 2 * P])

        bank = [ctx.enter_context(nc.psum_tensor(f"bank{k}", [P, 512], f32)) for k in range(8)]
        ps_eaT, ps_hotT_f, ps_h1, ps_msg1, ps_h2, ps_msg2, ps_agg = bank[0:7]
        ps_hotT = ps_hotT_f[0:3 * W, 0:CH // 2].bitcast(bf16)

        consts_landed = sem("consts_landed")
        N_CONST = 15 + 2 * TC
        dst_landed = sem("dst_landed")
        dstf_landed = sem("dstf_landed")
        zeroed = sem("zeroed")
        ident_set = sem("ident_set")
        ramps_set = sem("ramps_set")
        bn2_step = sem("bn2_step")
        range_set = sem("range_set")
        range_stored = sem("range_stored")
        range_back = sem("range_back")
        prep_step = sem("prep_step")
        ids_landed, weight_landed = sem("ids_landed"), sem("weight_landed")
        bn2_zeroed, ones_set, agg_zeroed = sem("bn2_zeroed"), sem("ones_set"), sem("agg_zeroed")
        rowid_set = sem("rowid_set")
        rowid_stored = sem("rowid_stored")
        passes_set = sem("passes_set")
        x_landed = slot_sems("x_landed", 2)
        stats_done, aggr_done, eps_added = sem("stats_done"), sem("aggr_done"), sem("eps_added")
        std_done, rstd_done, centred = sem("std_done"), sem("rstd_done"), sem("centred")
        scaled, h_done, res_done = sem("scaled"), sem("h_done"), sem("res_done")
        h_transposed, hT_copied = sem("h_transposed"), sem("hT_copied")
        pqr_ready, pqr_biased = sem("pqr_ready"), sem("pqr_biased")
        hi_done, res1_done, mid_done = sem("hi_done"), sem("res1_done"), sem("mid_done")
        res2_done, lo_done = sem("res2_done"), sem("lo_done")
        tables_stored = sem("tables_stored")
        agg_staged, agg_transposed, mid_added = sem("agg_staged"), sem("agg_transposed"), sem("mid_added")
        rel_ready, rel_biased = slot_sems("rel_ready", 2), slot_sems("rel_biased", 2)
        rel_stored = slot_sems("rel_stored", 2)
        agg_cleared = sem("agg_cleared")
        fin_relu, fin_added = sem("fin_relu"), sem("fin_added")
        out_stored = slot_sems("out_stored", 2)
        pass_ready = sem("pass_ready")
        pass_step = sem("pass_step")
        idx_landed, ea_landed = slot_sems("idx_landed"), slot_sems("ea_landed")
        qr_landed, prow_landed = slot_sems("qr_landed"), slot_sems("prow_landed")
        ea_transposed, h1_summed = slot_sems("ea_transposed"), slot_sems("h1_summed")
        h2_summed = slot_sems("h2_summed")
        hot_transposed, msg1_summed = sem("hot_transposed"), sem("msg1_summed")
        msg2_summed, chunk_summed = sem("msg2_summed"), sem("chunk_summed")
        eaT_copied, hotT_copied, hot_built = sem("eaT_copied"), sem("hotT_copied"), sem("hot_built")
        h1_done, agg_added = sem("h1_done"), sem("agg_added")
        msg1_done, h2_done, msg2_done = sem("msg1_done"), sem("h2_done"), sem("msg2_done")
        idx1_landed, rows_landed = slot_sems("idx1_landed"), slot_sems("rows_landed")
        hot1_built, rows_summed = sem("hot1_built"), slot_sems("rows_summed")
        agg1_added = slot_sems("agg1_added", 2)
        pass1_ready, pass1_step = sem("pass1_ready"), sem("pass1_step")

        block = ctx.enter_context(nc.Block())

        class Chunk:

            def __init__(self, m, quad, u):
                self.m, self.slot, q = m, u % SL, quad + u // SL
                self.i = q * SL + self.slot
                self.turn = m * (NCH // SL) + q
                self.n = m * NCH + self.i

        def all_chunks(eng, m, step):
            with eng.Fori(0, NCH // SL) as quad:
                for u in range(SL):
                    step(Chunk(m, quad, u))

        def pipelined(eng, m, head, step, tail):
            head(Chunk(m, 0, 0))
            with eng.Fori(0, NCH // SL - 1) as quad:
                for u in range(1, SL + 1):
                    step(Chunk(m, quad, u), Chunk(m, quad, u - 1), Chunk(m, quad, u + 1))
            q = NCH // SL - 1
            for u in range(1, SL):
                step(Chunk(m, q, u), Chunk(m, q, u - 1), Chunk(m, q, u + 1) if u < SL - 1 else None)
            tail(Chunk(m, q, SL - 1))

        def hold(eng):
            eng.nop(nofuse=True)

        def number_of_passes(eng):
            eng.wait_ge(passes_set, 1)
            return eng.value_load(passes_i[0:1, 0:1], min_val=1, max_val=MAXPASS)

        def window_start(eng, c):
            return eng.value_load(base_i[0:1, ds(c.i, 1)], min_val=0, max_val=TOP)

        def rel_buffer(it, b, j):
            tile = TPG * b + j
            return tile % 2, it * TPG + tile // 2

        def node_rows(t, group):
            return t[ds(group * (TPG * P), TPG * P), :].rearrange("(j p) d -> p j d", p=P)

        def wide(ap, n):
            p, a = ap.shape
            return ap.rearrange("p (a b) -> p a b", b=1).broadcast_to([p, a, n])

        def tiled(ap, n):
            p, a = ap.shape
            return ap.rearrange("p (b a) -> p b a", b=1).broadcast_to([p, n, a])

        @block.sync
        def _(sp):
            sp.dma_start(dst_rows[:, :, :], dst_c.rearrange("(q k) e -> q k e", q=QP)).then_inc(dst_landed, 16)
            sp.dma_start(rel_f[:, :].bitcast(i32), src_t).then_inc(ids_landed, 16)
            sp.dma_start(etype_i, etype_t).then_inc(ids_landed, 16)
            sp.dma_start(w_f[:, :], weight_t).then_inc(weight_landed, 16)
            sp.dma_start(dst_f[:, :].bitcast(i32), dst_t).then_inc(dstf_landed, 16)

            plain = [
                (w_node[:, 0:H1], we1[0:D, :]),
                (w_node[:, H1:2 * H1], we1[D:2 * D, :]),
                (w_node[:, 2 * H1:P], wn1[0:D, :]),
                (wn1_msg[:, :], wn1[D:2 * D, :]),
                (be2_col[:, :], be2.rearrange("(p o) -> p o", o=1)),
                (w_rel_sb[:, :, :], w_rel.rearrange("r f o -> f r o")),
                (b_rel_sb[:, :], b_rel.rearrange("r o -> (r o)").partition_broadcast(P)),
            ] + [(bn2_rep[:, t * D:(t + 1) * D], bn2.partition_broadcast(3 * W)) for t in range(TC)]
            in_zeros = [
                (bias_node[:, H1:2 * H1], be1.partition_broadcast(P)),
                (bias_node[:, 2 * H1:P], bn1.partition_broadcast(P)),
            ] + [
                (w1_pair[b * EA:(b + 1) * EA, q, (2 * q + b) * H1:(2 * q + b + 1) * H1], we1[2 * D:2 * D + EA, :])
                for q in range(2) for b in range(2)
            ] + [(w2_tile[j * H1:(j + 1) * H1, j, :], we2) for j in range(TC)] \
              + [(wn2_half[a * H2:(a + 1) * H2, a, :], wn2) for a in range(2)]
            assert len(plain) + len(in_zeros) == N_CONST
            for there, source in plain:
                sp.dma_start(there, source).then_inc(consts_landed, 16)
            sp.wait_ge(zeroed, 4)
            for there, source in in_zeros:
                sp.dma_start(there, source).then_inc(consts_landed, 16)

            sp.wait_ge(range_set, 3)
            sp.dma_start(base_d, least[:, :]).then_inc(range_stored, 16)
            sp.dma_start(range_d, most[:, :]).then_inc(range_stored, 16)
            sp.wait_ge(range_stored, 32)
            sp.dma_start(range_row[0:1, :], range_d.rearrange("q k -> (q k)").partition_broadcast(1)).then_inc(range_back, 16)
            sp.dma_start(base0[:, :], base_d.rearrange("q k -> (q k)").partition_broadcast(P)).then_inc(range_back, 16)
            sp.wait_ge(rowid_set, 1)
            sp.dma_start(row_tab, rel_f[:, :].bitcast(i32)).then_inc(rowid_stored, 16)

            def load_x(g, b):
                sp.dma_start(x_in[:, b, :, :], node_rows(x, g)).then_inc(x_landed[b], 16)

            def store_tables(g):
                sp.wait_ge(pqr_biased, 2 * g + 2)
                hold(sp)
                sp.wait_ge(lo_done, g + 1)
                hold(sp)
                sp.dma_start(node_rows(p_tab, g), pqr[:, :, 0:H1]).then_inc(tables_stored, 16)
                for t, part in zip(qr_tab, (qr_hi, qr_mid, qr_lo)):
                    sp.dma_start(node_rows(t, g), part[:, :, :]).then_inc(tables_stored, 16)

            load_x(0, 0)
            load_x(1, 1)
            with sp.Fori(0, NG // 2 - 1) as it:
                for b in range(2):
                    g = it * 2 + b
                    store_tables(g)
                    sp.wait_ge(res_done, g + 1)
                    hold(sp)
                    load_x(g + 2, b)
            for g in (NG - 2, NG - 1):
                store_tables(g)
            sp.wait_ge(tables_stored, 64 * NG)

            passes = number_of_passes(sp)

            def layer0_pass(m):
                sp.wait_ge(pass_ready, m + 1)
                hold(sp)

                def step(c):
                    s = c.slot
                    sp.wait_ge(prow_landed[s], c.turn * (16 * TC))
                    hold(sp)
                    sp.dma_start(idx[s][:, :], src_t[:, ds(c.i * TC, TC)]).then_inc(idx_landed[s], 16)
                    sp.wait_ge(ea_transposed[s], c.turn)
                    hold(sp)
                    sp.dma_start(ea[s][:, :], edge_attr[ds(c.i * CH, CH), :].rearrange("(p t) f -> p (t f)", t=TC))\
                      .then_inc(ea_landed[s], 16)
                    start = window_start(sp, c)
                    sp.wait_ge(h2_summed[s], c.turn)
                    hold(sp)
                    for k in range(3):
                        sp.dma_start(qr_w[s][k * W:(k + 1) * W, :], qr_tab[k][ds(start, W), :]).then_inc(qr_landed[s], 16)

                all_chunks(sp, m, step)

            with sp.Fori(0, passes) as m:
                layer0_pass(m)

            with sp.Fori(0, NTILE // 2) as it:
                for b in range(2):
                    sp.wait_ge(rel_biased[b], 2 * it + 2)
                    hold(sp)
                    sp.dma_start(rel_tab[ds((it * 2 + b) * (P * R), P * R), :].rearrange("(p r) o -> p (r o)", r=R),
                                 rel_rows[:, b, :]).then_inc(rel_stored[b], 16)
            for b in range(2):
                sp.wait_ge(rel_stored[b], 16 * (NTILE // 2))
            sp.wait_ge(rowid_stored, 16)

            passes = number_of_passes(sp)

            def layer1_pass(m):
                def step(c):
                    s = c.slot
                    sp.wait_ge(rows_landed[s], c.turn * (16 * TC))
                    hold(sp)
                    sp.dma_start(idx[s][:, :], row_tab[:, ds(c.i * TC, TC)]).then_inc(idx1_landed[s], 16)

                all_chunks(sp, m, step)

            sp.wait_ge(agg_cleared, 1)
            with sp.Fori(0, passes) as m:
                layer1_pass(m)

            with sp.Fori(0, NG // 2) as it:
                for b in range(2):
                    g = it * 2 + b
                    sp.wait_ge(fin_added, g + 1)
                    hold(sp)
                    sp.dma_start(node_rows(out, g), x_in[:, b, :, :]).then_inc(out_stored[b], 16)
            for b in range(2):
                sp.wait_ge(out_stored[b], 16 * (NG // 2))

        @block.gpsimd
        def _(pool):
            pool.memset(bias_node[:, 0:H1], 0.0).then_inc(zeroed, 1)
            pool.memset(w1_pair[:, :, :], 0.0).then_inc(zeroed, 1)
            pool.memset(w2_tile[:, :, :], 0.0).then_inc(zeroed, 1)
            pool.memset(wn2_half[:, :, :], 0.0).then_inc(zeroed, 1)
            pool.memset(bn2_rows[:, :], 0.0).then_inc(bn2_zeroed, 1)
            pool.memset(ones_b[:, :], 1.0).then_inc(ones_set, 1)
            pool.iota(iota_i[:, :], [[0, 3], [1, W]], base=0, channel_multiplier=0).then_inc(ramps_set, 1)
            pool.iota(pass_i[:, :], [[W, MAXPASS]], base=0, channel_multiplier=0).then_inc(ramps_set, 1)
            pool.memset(ident[:, :], 0.0).then_inc(ident_set, 1)
            pool.memset(ident_b[:, :], 0.0).then_inc(ident_set, 1)
            pool.wait_ge(ident_set, 2)
            for m in (ident, ident_b):
                pool.affine_select(out=m[:, :], in_=m[:, :], compare_op=ALU.not_equal, fill=1.0, base=0,
                                   pattern=[[-1, P]], channel_multiplier=1).then_inc(ident_set, 1)

            def gather(c, table, rows_of, used, idx_there, landed):
                s = c.slot
                pool.wait_ge(used[s], c.turn)
                hold(pool)
                pool.wait_ge(idx_there[s], 16 * c.turn + 16)
                hold(pool)
                for t in range(TC):
                    pool.indirect_dma_start(
                        out=rows_of[s][:, t, :], out_offset=None, in_=table,
                        in_offset=bass.IndirectOffsetOnAxis(ap=idx[s][:, t:t + 1], axis=0),
                    ).then_inc(landed[s], 16)

            pool.wait_ge(tables_stored, 64 * NG)
            passes = number_of_passes(pool)
            with pool.Fori(0, passes) as m:
                all_chunks(pool, m, lambda c: gather(c, p_tab, prow, h1_summed, idx_landed, prow_landed))

            for b in range(2):
                pool.wait_ge(rel_stored[b], 16 * (NTILE // 2))
            passes = number_of_passes(pool)
            with pool.Fori(0, passes) as m:
                all_chunks(pool, m, lambda c: gather(c, rel_tab, rows, rows_summed, idx1_landed, rows_landed))

        @block.scalar
        def _(act):
            def std_and_hT(k):
                act.wait_ge(eps_added, k + 1)
                act.activation(std[:, :], var_eps[:, :], ACT.Sqrt).then_inc(std_done, 1)
                act.wait_ge(h_transposed, 2 * k + 1)
                act.activation(hT[:, 0:4 * P], bank[0][:, 0:4 * P], ACT.Copy).then_inc(hT_copied, 1)
                act.wait_ge(h_transposed, 2 * k + 2)
                act.activation(hT[:, 4 * P:TPG * P], bank[1][:, 0:(TPG - 4) * P], ACT.Copy).then_inc(hT_copied, 1)

            with act.Fori(0, NG) as g:
                std_and_hT(g)
                act.wait_ge(pqr_biased, 2 * g + 2)
                act.wait_ge(tables_stored, 64 * g)
                act.activation(qr_hi[:, :, :], pqr[:, :, H1:P], ACT.Copy).then_inc(hi_done, 1)
                act.wait_ge(res1_done, g + 1)
                act.activation(qr_mid[:, :, :], qr_res[:, :, :], ACT.Copy).then_inc(mid_done, 1)

            def relu_h2(c):
                act.wait_ge(h2_summed[c.slot], c.turn + 1)
                act.activation(h2_sb[:, :], ps_h2[:, 0:2 * P], ACT.Relu).then_inc(h2_done, 1)

            def relu_msg2(c):
                act.wait_ge(msg2_summed, c.n + 1)
                act.activation(msg2_sb[:, :], ps_msg2[:, :], ACT.Relu).then_inc(msg2_done, 1)

            def relu_msg1(c):
                act.wait_ge(msg1_summed, c.n + 1)
                act.activation(msg1_sb[:, :], ps_msg1[:, :], ACT.Relu, bias=be2_col[:, 0:1]).then_inc(msg1_done, 1)

            act.wait_ge(consts_landed, 16 * N_CONST)
            passes = number_of_passes(act)

            def head(c):
                relu_msg1(c)

            def step(c, before, after):
                relu_h2(before)
                relu_msg2(before)
                relu_msg1(c)

            def tail(c):
                relu_h2(c)
                relu_msg2(c)

            with act.Fori(0, passes) as m:
                pipelined(act, m, head, step, tail)

            def stage_agg(k, g):
                act.wait_ge(agg_transposed, 2 * k)
                act.activation(agg_group[:, :], agg[:, ds(g * (TPG * P), TPG * P)], ACT.Copy).then_inc(agg_staged, 1)

            act.wait_ge(agg_added, passes * NCH)
            with act.Fori(0, NG) as g:
                stage_agg(g, g)
                std_and_hT(g + NG)

            for b in range(2):
                act.wait_ge(agg1_added[b], passes * (NCH // 2))
            with act.Fori(0, NG // 2) as it:
                for b in range(2):
                    g = it * 2 + b
                    stage_agg(g + NG, g)
                    act.wait_ge(out_stored[b], 16 * it)
                    for a, (t0, t1) in enumerate(((0, 4), (4, TPG))):
                        act.wait_ge(agg_transposed, 2 * (g + NG) + a + 1)
                        act.activation(x_in[:, b, t0:t1, :],
                                       bank[2 + a][:, 0:(t1 - t0) * P].rearrange("p (j d) -> p j d", d=D), ACT.Relu)\
                           .then_inc(fin_relu, 1)

        @block.vector
        def _(dve):
            dve.wait_ge(dst_landed, 16)
            dve.tensor_reduce(least[:, :], dst_rows[:, :, :].bitcast(u32), AX.X, ALU.min).then_inc(range_set, 1)
            dve.tensor_reduce(most[:, :], dst_rows[:, :, :], AX.X, ALU.max).then_inc(range_set, 1)
            dve.wait_ge(range_set, 2)
            dve.tensor_tensor(most[:, :], most[:, :], least[:, :], ALU.subtract).then_inc(range_set, 1)
            dve.wait_ge(ids_landed, 32)
            dve.scalar_tensor_tensor(out=rel_f[:, :].bitcast(i32), in0=rel_f[:, :].bitcast(i32), scalar=float(R),
                                     in1=etype_i, op0=ALU.mult, op1=ALU.add).then_inc(rowid_set, 1)
            dve.wait_ge(dstf_landed, 16)
            dve.tensor_copy(dst_f[:, :], dst_f[:, :].bitcast(i32)).then_inc(prep_step, 1)
            dve.wait_ge(ramps_set, 2)
            dve.tensor_copy(iota_f[:, :], iota_i[:, :]).then_inc(prep_step, 1)
            dve.tensor_copy(pass_f[:, :], pass_i[:, :]).then_inc(prep_step, 1)
            dve.wait_ge(consts_landed, 16 * N_CONST)
            dve.wait_ge(bn2_zeroed, 1)
            source = bn2_rep
            for k in range(3):
                dve.tensor_copy(bn2_part[:, :], source[:, :]).then_inc(bn2_step, 1)
                dve.wait_ge(bn2_step, 3 * k + 1)
                dve.tensor_copy(bn2_rows[k * W:k * W + 1, :], bn2_part[k * W:k * W + 1, :]).then_inc(bn2_step, 1)
                dve.tensor_tensor(bn2_res[:, :], source[:, :], bn2_part[:, :], ALU.subtract).then_inc(bn2_step, 1)
                dve.wait_ge(bn2_step, 3 * k + 3)
                source = bn2_res
            dve.wait_ge(range_back, 32)
            dve.tensor_reduce(range_max[:, :], range_row[:, :], AX.X, ALU.max).then_inc(prep_step, 1)
            dve.tensor_scalar_add(base0[:, :], base0[:, :], -float(W)).then_inc(prep_step, 1)
            dve.wait_ge(prep_step, 5)
            dve.tensor_scalar(pass_f[:, :], pass_f[:, :], range_max[0:1, 0:1], None, ALU.is_le).then_inc(prep_step, 1)
            dve.wait_ge(prep_step, 6)
            dve.tensor_reduce(passes_f[:, :], pass_f[:, :], AX.X, ALU.add).then_inc(prep_step, 1)
            dve.wait_ge(prep_step, 7)
            dve.tensor_copy(passes_i[:, :], passes_f[:, :]).then_inc(passes_set, 1)

            def layer_norm(k, source):
                for j in range(TPG):
                    ins = dve.bn_stats(stats[:, j, :], source(j))
                ins.then_inc(stats_done, 1)
                dve.wait_ge(stats_done, k + 1)
                hold(dve)
                for j in range(TPG):
                    ins = dve.bn_aggr(mv[:, j, :], stats[:, j, :])
                ins.then_inc(aggr_done, 1)
                dve.wait_ge(aggr_done, k + 1)
                dve.tensor_scalar_add(var_eps[:, :], mv[:, :, 1], EPS).then_inc(eps_added, 1)
                dve.wait_ge(h_transposed, 2 * k)
                dve.tensor_tensor(h[:, :, :], source(None), wide(mv[:, :, 0], D), ALU.subtract).then_inc(centred, 1)
                dve.wait_ge(std_done, k + 1)
                dve.reciprocal(rstd[:, :], std[:, :]).then_inc(rstd_done, 1)
                dve.wait_ge(rstd_done, k + 1)
                dve.wait_ge(centred, k + 1)
                dve.scalar_tensor_tensor(out=h[:, :, :], in0=h[:, :, :], scalar=0.0, in1=wide(rstd[:, :], D),
                                         op0=ALU.max, op1=ALU.mult).then_inc(h_done, 1)

            with dve.Fori(0, NG // 2) as it:
                for b in range(2):
                    g = it * 2 + b
                    dve.wait_ge(x_landed[b], 16 * it + 16)
                    layer_norm(g, lambda j: x_in[:, b, :, :] if j is None else x_in[:, b, j, :])
                    dve.wait_ge(h_done, g + 1)
                    dve.tensor_tensor(res[:, ds(g * TPG, TPG), :], h[:, :, :], x_in[:, b, :, :], ALU.add)\
                       .then_inc(res_done, 1)
                    dve.wait_ge(tables_stored, 64 * g)
                    for a, (t0, t1) in enumerate(((0, 4), (4, TPG))):
                        dve.wait_ge(pqr_ready, 2 * g + a + 1)
                        dve.tensor_tensor(pqr[:, t0:t1, :],
                                          bank[2 + a][:, 0:(t1 - t0) * P].rearrange("p (j d) -> p j d", d=P),
                                          tiled(bias_node[:, :], t1 - t0), ALU.add).then_inc(pqr_biased, 1)
                    dve.wait_ge(hi_done, g + 1)
                    dve.tensor_tensor(qr_res[:, :, :], pqr[:, :, H1:P], qr_hi[:, :, :], ALU.subtract).then_inc(res1_done, 1)
                    dve.wait_ge(mid_done, g + 1)
                    dve.tensor_tensor(qr_lo[:, :, :], qr_res[:, :, :], qr_mid[:, :, :], ALU.subtract).then_inc(lo_done, 1)

            def set_windows(m, step, ready):
                dve.tensor_scalar_add(base_f[:, :], base_f[:, :], float(W)).then_inc(step, 1)
                dve.wait_ge(step, 2 * m + 1)
                dve.tensor_scalar_min(base_i[:, :], base_f[:, :], float(TOP)).then_inc(step, 1)
                dve.wait_ge(step, 2 * m + 2)
                dve.tensor_tensor(rel_f[:, :].rearrange("p (c t) -> p c t", t=TC), dst_f[:, :].rearrange("p (c t) -> p c t", t=TC),
                                  wide(base_i[:, :], TC), ALU.subtract).then_inc(ready, 1)

            dve.wait_ge(rowid_stored, 16)
            dve.memset(agg[:, :], 0.0).then_inc(agg_zeroed, 1)
            dve.wait_ge(agg_zeroed, 1)
            dve.tensor_copy(base_f[:, :], base0[:, :]).then_inc(prep_step, 1)
            dve.wait_ge(prep_step, 8)
            passes = number_of_passes(dve)

            def build_hot(c):
                offset = rel_f[:, ds(c.i * TC, TC)]
                dve.tensor_tensor(hot3[c.slot][:, :, :], tiled(iota_f[:, :], TC), wide(offset, 3 * W), ALU.is_equal)
                dve.tensor_tensor(hot[c.slot][:, :, :], tiled(iota_f[:, 0:W], TC), wide(offset, W), ALU.is_equal)\
                   .then_inc(hot_built, 1)

            def copy_transposes(c):
                dve.wait_ge(ea_transposed[c.slot], c.turn + 1)
                dve.tensor_copy(eaT[:, :], ps_eaT[:, 0:2 * P]).then_inc(eaT_copied, 1)
                dve.wait_ge(hot_transposed, c.n + 1)
                dve.tensor_copy(hotT[c.slot % 2][:, :], ps_hotT).then_inc(hotT_copied, 1)

            def relu_h1(c):
                dve.wait_ge(h1_summed[c.slot], c.turn + 1)
                dve.tensor_scalar_max(h1_sb[:, :], ps_h1[:, 0:P], 0.0).then_inc(h1_done, 1)

            def add_chunk(c):
                start = window_start(dve, c)
                dve.wait_ge(chunk_summed, c.n + 1)
                dve.wait_ge(agg_added, c.n)
                dve.tensor_tensor(agg[:, ds(start, W)], agg[:, ds(start, W)], ps_agg[:, 0:W], ALU.add).then_inc(agg_added, 1)

            def head(c):
                build_hot(c)
                copy_transposes(c)
                build_hot(Chunk(c.m, 0, 1))
                relu_h1(c)

            def step(c, before, after):
                copy_transposes(c)
                if after is not None:
                    build_hot(after)
                relu_h1(c)
                add_chunk(before)

            with dve.Fori(0, passes) as m:
                dve.wait_ge(chunk_summed, m * NCH)
                set_windows(m, pass_step, pass_ready)
                dve.wait_ge(pass_ready, m + 1)
                hold(dve)
                pipelined(dve, m, head, step, add_chunk)

            with dve.Fori(0, NG // 2) as it:
                for b in range(2):
                    g = it * 2 + b
                    for a, (t0, t1) in enumerate(((0, 4), (4, TPG))):
                        there = res[:, ds(g * TPG + t0, t1 - t0), :]
                        dve.wait_ge(agg_transposed, 2 * g + a + 1)
                        dve.tensor_tensor(there, there, bank[2 + a][:, 0:(t1 - t0) * P].rearrange("p (j d) -> p j d", d=D),
                                          ALU.add).then_inc(mid_added, 1)
                    dve.wait_ge(mid_added, 2 * g + 2)
                    hold(dve)
                    layer_norm(g + NG, lambda j: res[:, ds(g * TPG, TPG), :] if j is None else
                               res[:, ds(g * TPG + j, 1), :].rearrange("p j d -> p (j d)"))
                    for j in range(TPG):
                        buf, turn = rel_buffer(it, b, j)
                        dve.wait_ge(rel_stored[buf], 16 * turn)
                        for a in range(2):
                            dve.wait_ge(rel_ready[buf], 2 * turn + a + 1)
                            cols = slice(a * 512, a * 512 + 512)
                            dve.tensor_tensor(rel_rows[:, buf, cols], bank[4 + 2 * buf + a][:, :], b_rel_sb[:, cols], ALU.add)\
                               .then_inc(rel_biased[buf], 1)

            dve.wait_ge(agg_staged, NG)
            dve.memset(agg[:, :], 0.0).then_inc(agg_cleared, 1)
            dve.wait_ge(agg_cleared, 1)
            dve.wait_ge(weight_landed, 16)
            dve.tensor_copy(base_f[:, :], base0[:, :]).then_inc(prep_step, 1)
            dve.wait_ge(prep_step, 9)

            with dve.Fori(0, passes) as m:
                for s in range(SL):
                    dve.wait_ge(rows_summed[s], m * (NCH // SL))
                set_windows(m, pass1_step, pass1_ready)
                dve.wait_ge(pass1_ready, m + 1)
                hold(dve)

                def step(c):
                    s = c.slot
                    dve.wait_ge(rows_summed[s], c.turn)
                    for t in range(TC):
                        at = ds(c.i * TC + t, 1)
                        ins = dve.tensor_scalar(hot[s][:, t, :], iota_f[:, 0:W], rel_f[:, at], w_f[:, at],
                                                ALU.is_equal, ALU.mult)
                    ins.then_inc(hot1_built, 1)
                    start = window_start(dve, c)
                    dve.wait_ge(rows_summed[s], c.turn + 1)
                    dve.wait_ge(agg1_added[1 - s % 2], 2 * c.turn + (s + 1) // 2)
                    dve.tensor_tensor(agg[:, ds(start, W)], agg[:, ds(start, W)], bank[6 + s % 2][:, 0:W], ALU.add)\
                       .then_inc(agg1_added[s % 2], 1)

                all_chunks(dve, m, step)

            with dve.Fori(0, NG // 2) as it:
                for b in range(2):
                    g = it * 2 + b
                    dve.wait_ge(fin_relu, 2 * g + 2)
                    dve.tensor_tensor(x_in[:, b, :, :], x_in[:, b, :, :], res[:, ds(g * TPG, TPG), :], ALU.add)\
                       .then_inc(fin_added, 1)

        @block.tensor
        def _(pe):
            pe.wait_ge(ident_set, 4)
            pe.wait_ge(consts_landed, 16 * N_CONST)
            pe.wait_ge(ones_set, 1)
            pe.wait_ge(bn2_step, 9)
            HALVES = ((0, 4), (4, TPG))

            def transpose_h(k):
                pe.wait_ge(h_done, k + 1)
                pe.wait_ge(hT_copied, 2 * k)
                for a, (t0, t1) in enumerate(HALVES):
                    for j in range(t0, t1):
                        ins = pe.transpose(bank[a][:, (j - t0) * P:(j - t0 + 1) * P], h[:, j, :], ident[:, :])
                    ins.then_inc(h_transposed, 1)

            def transpose_agg(k, free):
                pe.wait_ge(agg_staged, k + 1)
                free()
                for a, (t0, t1) in enumerate(HALVES):
                    for j in range(t0, t1):
                        ins = pe.transpose(bank[2 + a][:, (j - t0) * P:(j - t0 + 1) * P],
                                           agg_group[:, j * P:(j + 1) * P], ident[:, :])
                    ins.then_inc(agg_transposed, 1)

            with pe.Fori(0, NG) as g:
                transpose_h(g)
                pe.wait_ge(pqr_biased, 2 * g)
                for a, (t0, t1) in enumerate(HALVES):
                    pe.wait_ge(hT_copied, 2 * g + a + 1)
                    for j in range(t0, t1):
                        ins = pe.matmul(bank[2 + a][:, (j - t0) * P:(j - t0 + 1) * P],
                                        hT[:, j * P:(j + 1) * P], w_node[:, :], start=True, stop=True)
                    ins.then_inc(pqr_ready, 1)

            def transposes(c):
                s = c.slot
                pe.wait_ge(ea_landed[s], 16 * c.turn + 16)
                pe.wait_ge(eaT_copied, c.n)
                for q in range(2):
                    ins = pe.transpose(ps_eaT[:, q * P:(q + 1) * P], ea[s][:, q * P:(q + 1) * P], ident[:, :])
                ins.then_inc(ea_transposed[s], 1)
                pe.wait_ge(hot_built, c.n + 1)
                pe.wait_ge(hotT_copied, c.n)
                for t in range(TC):
                    ins = pe.transpose(ps_hotT[:, t * P:(t + 1) * P], hot3[s][:, t, :], ident_b[:, :])
                ins.then_inc(hot_transposed, 1)

            def sum_h1(c):
                s = c.slot
                pe.wait_ge(h1_done, c.n)
                pe.wait_ge(eaT_copied, c.n + 1)
                for q in range(2):
                    pe.matmul(ps_h1[:, 0:P], w1_pair[:, q, :], eaT[:, q * P:(q + 1) * P], start=(q == 0), stop=False)
                pe.wait_ge(qr_landed[s], 48 * c.turn + 48)
                pe.wait_ge(hotT_copied, c.n + 1)
                for t in range(TC):
                    pe.matmul(ps_h1[t * H1:(t + 1) * H1, 0:P], qr_w[s][:, 0:H1], hotT[s % 2][:, t * P:(t + 1) * P],
                              start=False, stop=False)
                pe.wait_ge(prow_landed[s], 16 * TC * c.turn + 16 * TC)
                pe.matmul(ps_h1[:, 0:P], prow[s][:, :, :].rearrange("p t o -> p (t o)"), ident[:, :], start=False, stop=True)\
                  .then_inc(h1_summed[s], 1)

            def sum_msg1(c):
                pe.wait_ge(msg1_done, c.n)
                pe.wait_ge(h1_done, c.n + 1)
                for t in range(TC):
                    ins = pe.matmul(ps_msg1[:, t * P:(t + 1) * P], w2_tile[:, t, :], h1_sb[:, :], start=True, stop=True)
                ins.then_inc(msg1_summed, 1)

            def sum_h2(c):
                s = c.slot
                pe.wait_ge(h2_done, c.n)
                pe.wait_ge(msg1_done, c.n + 1)
                for a in range(2):
                    there = ps_h2[a * H2:(a + 1) * H2, 0:2 * P]
                    cols = slice(a * 2 * P, (a + 1) * 2 * P)
                    pe.matmul(there, wn1_msg[:, :], msg1_sb[:, cols], start=True, stop=False)
                    ins = pe.matmul(there, qr_w[s][:, H1:QR], hotT[s % 2][:, cols], start=False, stop=True)
                ins.then_inc(h2_summed[s], 1)

            def sum_msg2(c):
                pe.wait_ge(msg2_done, c.n)
                pe.wait_ge(h2_done, c.n + 1)
                pe.matmul(ps_msg2[:, :], ones_b[:, :], bn2_rows[:, :], start=True, stop=False)
                for t in range(TC):
                    a, b = t // 2, t % 2
                    ins = pe.matmul(ps_msg2[:, t * P:(t + 1) * P], h2_sb[:, b * P:(b + 1) * P], wn2_half[:, a, :],
                                    start=False, stop=(t == TC - 1))
                ins.then_inc(msg2_summed, 1)

            def sum_chunk(c):
                pe.wait_ge(agg_added, c.n)
                pe.wait_ge(msg2_done, c.n + 1)
                for t in range(TC):
                    ins = pe.matmul(ps_agg[:, 0:W], msg2_sb[:, t * P:(t + 1) * P], hot[c.slot][:, t, :],
                                    start=(t == 0), stop=(t == TC - 1))
                ins.then_inc(chunk_summed, 1)

            passes = number_of_passes(pe)

            def head(c):
                transposes(c)
                sum_h1(c)
                sum_msg1(c)

            def step(c, before, after):
                transposes(c)
                sum_h2(before)
                sum_h1(c)
                sum_msg2(before)
                sum_msg1(c)
                sum_chunk(before)

            def tail(c):
                sum_h2(c)
                sum_msg2(c)
                sum_chunk(c)

            with pe.Fori(0, passes) as m:
                pipelined(pe, m, head, step, tail)

            with pe.Fori(0, NG // 2) as it:
                for b in range(2):
                    g = it * 2 + b
                    transpose_agg(g, lambda: pe.wait_ge(mid_added, 2 * g))
                    transpose_h(g + NG)
                    pe.wait_ge(hT_copied, 2 * (g + NG) + 2)
                    for j in range(TPG):
                        buf, turn = rel_buffer(it, b, j)
                        pe.wait_ge(rel_biased[buf], 2 * turn)
                        for a in range(2):
                            pe.matmul(bank[4 + 2 * buf + a][:, :], hT[:, j * P:(j + 1) * P],
                                      w_rel_sb[:, a * R // 2:(a + 1) * R // 2, :].rearrange("f r o -> f (r o)"),
                                      start=True, stop=True).then_inc(rel_ready[buf], 1)

            def step1(c):
                s = c.slot
                pe.wait_ge(hot1_built, c.n + 1)
                pe.wait_ge(rows_landed[s], 16 * TC * c.turn + 16 * TC)
                pe.wait_ge(agg1_added[s % 2], 2 * c.turn + s // 2)
                for t in range(TC):
                    ins = pe.matmul(bank[6 + s % 2][:, 0:W], rows[s][:, t, :], hot[s][:, t, :],
                                    start=(t == 0), stop=(t == TC - 1))
                ins.then_inc(rows_summed[s], 1)

            with pe.Fori(0, passes) as m:
                all_chunks(pe, m, step1)

            with pe.Fori(0, NG) as g:
                transpose_agg(g + NG, lambda: pe.wait_ge(fin_relu, 2 * g))

    return nc


def kernel(x, src, dst, edge_attr_64, edge_type_8, edge_weight1, L0_gnn_We1, L0_gnn_be1, L0_gnn_We2, L0_gnn_be2,
           L0_gnn_Wn1, L0_gnn_bn1, L0_gnn_Wn2, L0_gnn_bn2, L1_gnn_W, L1_gnn_b):
    import numpy as np
    import concourse.bacc as bacc
    from concourse import mybir
    from concourse.bass_utils import run_bass_kernel_spmd

    nodes, width = x.shape
    edges = src.shape[0]
    group, chunk, tiles, block = 2 * 7 * 128, 512, 4, 4 * 512
    n_pad = -(-nodes // group) * group - nodes
    e_pad = -(-edges // block) * block - edges
    n_chunks = (edges + e_pad) // chunk

    def padded(a, n, value=0):
        a = np.asarray(a)
        return np.concatenate([a, np.full((n,) + a.shape[1:], value, a.dtype)])

    def by_partition(a):
        return np.ascontiguousarray(a.reshape(n_chunks, chunk // tiles, tiles).transpose(1, 0, 2).reshape(chunk // tiles, -1))

    dst_pad = padded(dst, e_pad, -1)
    arrays = {
        "x": padded(x, n_pad),
        "src_t": by_partition(padded(src, e_pad)),
        "dst_t": by_partition(dst_pad),
        "etype_t": by_partition(padded(edge_type_8, e_pad)),
        "weight_t": by_partition(padded(np.asarray(edge_weight1)[:, 0], e_pad)),
        "dst_c": dst_pad.reshape(n_chunks, chunk),
        "edge_attr": padded(edge_attr_64, e_pad),
        "we1": L0_gnn_We1, "be1": L0_gnn_be1, "we2": L0_gnn_We2, "be2": L0_gnn_be2,
        "wn1": L0_gnn_Wn1, "bn1": L0_gnn_bn1, "wn2": L0_gnn_Wn2, "bn2": L0_gnn_bn2,
        "w_rel": L1_gnn_W, "b_rel": L1_gnn_b,
    }
    arrays = {f"in_{k}": np.ascontiguousarray(a) for k, a in arrays.items()}
    nc = bacc.Bacc("TRN2", target_bir_lowering=False, num_devices=1)
    args = [nc.dram_tensor(k, a.shape, mybir.dt.from_np(a.dtype), kind="ExternalInput").ap() for k, a in arrays.items()]
    args.append(nc.dram_tensor("out_x", [nodes + n_pad, width], mybir.dt.float32, kind="ExternalOutput").ap())
    gnn_two_layers(nc, *args)
    got = run_bass_kernel_spmd(nc, [arrays], core_ids=[0])
    return got.results[0]["out_x"][:nodes]
```

```python
import concourse.bass as bass
from concourse import mybir
from contextlib import ExitStack


def gnn_two_layers(nc, x, src_t, dst_t, etype_t, weight_t, dst_c, edge_cols,
                   we1, be1, we2, be2, wn1, bn1, wn2, bn2, w_rel, b_rel, out):
    f32, bf16, i32, u32 = mybir.dt.float32, mybir.dt.bfloat16, mybir.dt.int32, mybir.dt.uint32
    ALU, ACT, AX = mybir.AluOpType, mybir.ActivationFunctionType, mybir.AxisListType
    ds = bass.ds

    P = 128
    NPAD, D = x.shape
    TPG = 7
    NG = NPAD // (P * TPG)
    NTILE = NG * TPG
    TC = 4
    CH = TC * P
    NCH = dst_c.shape[0]
    SL = 4
    W = 32
    EA = edge_cols.shape[1] // 2
    H1 = we2.shape[0]
    H2 = wn2.shape[0]
    QR = H1 + H2
    R = w_rel.shape[0]
    MAXPASS = (NPAD + W - 1) // W
    TOP = NPAD - W
    EPS = 1e-5
    assert NG % 2 == 0 and NCH % SL == 0 and TC * H1 == P and 2 * H2 == P and 2 * EA == P and 3 * W <= P
    QP = max(q for q in range(1, P + 1) if NCH % q == 0)
    QC = NCH // QP

    p_tab = nc.dram_tensor("p_tab", [NPAD, H1], f32).ap()
    qr_tab = [nc.dram_tensor(f"qr_tab{k}", [NPAD, QR], bf16).ap() for k in range(3)]
    rel_tab = nc.dram_tensor("rel_tab", [NPAD * R, D], f32).ap()
    row_tab = nc.dram_tensor("row_tab", [P, NCH * TC], i32).ap()
    base_d = nc.dram_tensor("base_d", [QP, QC], f32).ap()
    range_d = nc.dram_tensor("range_d", [QP, QC], f32).ap()

    ctx = ExitStack()
    with ctx:
        def sb(name, shape, dt=f32):
            return ctx.enter_context(nc.sbuf_tensor(name, shape, dt))

        def sem(name):
            return ctx.enter_context(nc.semaphore(name))

        def slot_sems(name, n=SL):
            return [sem(f"{name}{k}") for k in range(n)]

        w_node = sb("w_node", [P, P])
        bias_node = sb("bias_node", [P, P])
        w1_pair = sb("w1_pair", [P, 2, P])
        w2_tile = sb("w2_tile", [P, TC, P])
        wn1_msg = sb("wn1_msg", [P, H2])
        wn2_half = sb("wn2_half", [P, 2, P])
        be2_col = sb("be2_col", [P, 1])
        bn2_rep = sb("bn2_rep", [P, TC * D])
        w_rel_sb = sb("w_rel_sb", [P, R, D])
        b_rel_sb = sb("b_rel_sb", [P, R * D])
        ident = sb("ident", [P, P])
        fold_tiles = sb("fold_tiles", [P, W])
        iota_i = sb("iota_i", [P, W], i32)
        iota_f = sb("iota_f", [P, W])
        row_i = sb("row_i", [3 * W, 1], i32)
        row_f = sb("row_f", [3 * W, 1])

        dst_f = sb("dst_f", [P, NCH * TC])
        rel_f = sb("rel_f", [P, NCH * TC])
        w_f = sb("w_f", [P, NCH * TC])
        least = sb("least", [QP, QC])
        most = sb("most", [QP, QC])
        base0 = sb("base0", [P, NCH])
        base_f = sb("base_f", [P, NCH])
        base_c = sb("base_c", [P, NCH])
        base_i = sb("base_i", [P, NCH], i32)
        range_max = sb("range_max", [1, 1])
        passes_f = sb("passes_f", [1, 1])
        passes_i = sb("passes_i", [1, 1], i32)

        res = sb("res", [P, NTILE, D])
        agg = sb("agg", [P, NPAD])
        taken = 0

        def in_agg(n, parts=P):
            nonlocal taken
            taken += n
            assert taken <= NPAD
            return agg[0:parts, taken - n:taken]

        dst_rows = in_agg(QC * CH, QP).bitcast(i32).rearrange("q (k e) -> q k e", e=CH)
        etype_i = in_agg(NCH * TC).bitcast(i32)
        range_row = in_agg(NCH, 1)
        pass_i = in_agg(MAXPASS, 1).bitcast(i32)
        pass_f = in_agg(MAXPASS, 1)
        x_in = sb("x_in", [P, 2, TPG, D])
        h = sb("h", [P, TPG, D])
        hT = sb("hT", [P, TPG * P])
        stats = sb("stats", [P, TPG, 6])
        mv = sb("mv", [P, TPG, 2])
        var_eps = sb("var_eps", [P, TPG])
        std = sb("std", [P, TPG])
        rstd = sb("rstd", [P, TPG])
        agg_group = sb("agg_group", [P, TPG * P])
        shared = sb("shared", [P, max(TPG * (P + QR) + 3 * TPG * QR // 2, SL * TC * (EA + H1) + 2 * CH)])
        taken_by = {"tables": 0, "edges": 0}

        def in_shared(who, n):
            taken_by[who] += n
            return shared[:, taken_by[who] - n:taken_by[who]]

        pqr = in_shared("tables", TPG * P).rearrange("p (j d) -> p j d", d=P)
        qr_res = in_shared("tables", TPG * QR).rearrange("p (j d) -> p j d", d=QR)
        qr_hi, qr_mid, qr_lo = (in_shared("tables", TPG * QR // 2).bitcast(bf16).rearrange("p (j d) -> p j d", d=QR)
                                for _ in range(3))
        ea = [in_shared("edges", TC * EA) for s in range(SL)]
        prow = [in_shared("edges", TC * H1).rearrange("p (t o) -> p t o", o=H1) for s in range(SL)]
        msg1_sb, msg2_sb = (in_shared("edges", CH) for _ in range(2))
        rel_place = sb("rel_place", [P, max(2 * R * D, SL * TC * D)])
        rel_rows = rel_place[:, 0:2 * R * D].rearrange("p (b n) -> p b n", b=2)
        dst_wide = [rel_place[0:3 * W, s * CH:(s + 1) * CH].bitcast(i32) for s in range(SL)]
        rows = [rel_place[:, s * TC * D:(s + 1) * TC * D].rearrange("p (t d) -> p t d", d=D) for s in range(SL)]

        idx = [sb(f"idx{s}", [P, TC], i32) for s in range(SL)]
        qr_w = [sb(f"qr_w{s}", [3 * W, QR], bf16) for s in range(SL)]
        hot = [sb(f"hot{s}", [P, TC, W]) for s in range(SL)]
        hotT = [sb(f"hotT{s}", [3 * W, CH], bf16) for s in range(2)]
        h1_sb = sb("h1_sb", [P, P])
        h2_sb = sb("h2_sb", [P, 2 * P])
        tile_sums = sb("tile_sums", [P, D])

        bank = [ctx.enter_context(nc.psum_tensor(f"bank{k}", [P, 512], f32)) for k in range(8)]
        ps_h1, ps_msg1, ps_h2, ps_msg2, ps_tiles, ps_agg = bank[0:6]

        consts_landed = sem("consts_landed")
        N_CONST = 15 + 2 * TC
        dst_landed = sem("dst_landed")
        dstf_landed = sem("dstf_landed")
        zeroed = sem("zeroed")
        ident_set = sem("ident_set")
        ramps_set = sem("ramps_set")
        fold_step = sem("fold_step")
        range_set = sem("range_set")
        range_stored = sem("range_stored")
        range_back = sem("range_back")
        prep_step = sem("prep_step")
        ids_landed, weight_landed = sem("ids_landed"), sem("weight_landed")
        rowid_set = sem("rowid_set")
        rowid_stored = sem("rowid_stored")
        passes_set = sem("passes_set")
        x_landed = slot_sems("x_landed", 2)
        stats_done, aggr_done, eps_added = sem("stats_done"), sem("aggr_done"), sem("eps_added")
        std_done, rstd_done, centred = sem("std_done"), sem("rstd_done"), sem("centred")
        scaled, h_done, res_done = sem("scaled"), sem("h_done"), sem("res_done")
        h_transposed, hT_copied = sem("h_transposed"), sem("hT_copied")
        pqr_ready, pqr_biased = sem("pqr_ready"), sem("pqr_biased")
        hi_done, res1_done, mid_done = sem("hi_done"), sem("res1_done"), sem("mid_done")
        res2_done, lo_done = sem("res2_done"), sem("lo_done")
        tables_stored = sem("tables_stored")
        agg_staged, agg_transposed, mid_added = sem("agg_staged"), sem("agg_transposed"), sem("mid_added")
        rel_ready, rel_biased = slot_sems("rel_ready", 2), slot_sems("rel_biased", 2)
        rel_stored = slot_sems("rel_stored", 2)
        agg_cleared = sem("agg_cleared")
        fin_relu, fin_added = sem("fin_relu"), sem("fin_added")
        out_stored = slot_sems("out_stored", 2)
        pass_ready = sem("pass_ready")
        pass_step = sem("pass_step")
        idx_landed, ea_landed = slot_sems("idx_landed"), slot_sems("ea_landed")
        qr_landed, prow_landed = slot_sems("qr_landed"), slot_sems("prow_landed")
        dst_wide_landed = slot_sems("dst_wide_landed")
        h1_summed, h2_summed, hot_built = slot_sems("h1_summed"), slot_sems("h2_summed"), slot_sems("hot_built")
        msg1_summed, msg2_summed = sem("msg1_summed"), sem("msg2_summed")
        tiles_summed, chunk_summed = sem("tiles_summed"), sem("chunk_summed")
        h1_done, msg1_done, h2_done = sem("h1_done"), sem("msg1_done"), sem("h2_done")
        msg2_biased, msg2_done = sem("msg2_biased"), sem("msg2_done")
        tiles_copied, agg_added = sem("tiles_copied"), sem("agg_added")
        idx1_landed, rows_landed = slot_sems("idx1_landed"), slot_sems("rows_landed")
        hot1_built, rows_summed = sem("hot1_built"), slot_sems("rows_summed")
        agg1_added = slot_sems("agg1_added", 2)
        pass1_ready, pass1_step = sem("pass1_ready"), sem("pass1_step")

        block = ctx.enter_context(nc.Block())

        class Chunk:

            def __init__(self, m, quad, u):
                self.m, self.slot, q = m, u % SL, quad + u // SL
                self.i = q * SL + self.slot
                self.turn = m * (NCH // SL) + q
                self.n = m * NCH + self.i

        def all_chunks(eng, m, step):
            with eng.Fori(0, NCH // SL) as quad:
                for u in range(SL):
                    step(Chunk(m, quad, u))

        def pipelined(m_, eng, step):
            Q = NCH // SL
            at = lambda quad, u: Chunk(m_, quad, u)
            step(at(0, 0), None, None, at(0, 1))
            step(at(0, 1), at(0, 0), None, at(0, 2))
            with eng.Fori(0, Q - 1) as quad:
                for u in range(2, SL + 2):
                    step(at(quad, u), at(quad, u - 1), at(quad, u - 2), at(quad, u + 1))
            step(at(Q - 1, 2), at(Q - 1, 1), at(Q - 1, 0), at(Q - 1, 3))
            step(at(Q - 1, 3), at(Q - 1, 2), at(Q - 1, 1), None)
            step(None, at(Q - 1, 3), at(Q - 1, 2), None)
            step(None, None, at(Q - 1, 3), None)

        def hold(eng):
            eng.nop(nofuse=True)

        def number_of_passes(eng):
            eng.wait_ge(passes_set, 1)
            return eng.value_load(passes_i[0:1, 0:1], min_val=1, max_val=MAXPASS)

        def window_start(eng, c):
            return eng.value_load(base_i[0:1, ds(c.i, 1)], min_val=0, max_val=TOP)

        def rel_buffer(it, b, j):
            tile = TPG * b + j
            return tile % 2, it * TPG + tile // 2

        def node_rows(t, group):
            return t[ds(group * (TPG * P), TPG * P), :].rearrange("(j p) d -> p j d", p=P)

        def wide(ap, n):
            p, a = ap.shape
            return ap.rearrange("p (a b) -> p a b", b=1).broadcast_to([p, a, n])

        def tiled(ap, n):
            p, a = ap.shape
            return ap.rearrange("p (b a) -> p b a", b=1).broadcast_to([p, n, a])

        @block.sync
        def _(sp):
            sp.dma_start(dst_rows[:, :, :], dst_c.rearrange("(q k) e -> q k e", q=QP)).then_inc(dst_landed, 16)
            sp.dma_start(rel_f[:, :].bitcast(i32), src_t).then_inc(ids_landed, 16)
            sp.dma_start(etype_i, etype_t).then_inc(ids_landed, 16)
            sp.dma_start(w_f[:, :], weight_t).then_inc(weight_landed, 16)
            sp.dma_start(dst_f[:, :].bitcast(i32), dst_t).then_inc(dstf_landed, 16)

            plain = [
                (w_node[:, 0:H1], we1[0:D, :]),
                (w_node[:, H1:2 * H1], we1[D:2 * D, :]),
                (w_node[:, 2 * H1:P], wn1[0:D, :]),
                (wn1_msg[:, :], wn1[D:2 * D, :]),
                (be2_col[:, :], be2.rearrange("(p o) -> p o", o=1)),
                (w_rel_sb[:, :, :], w_rel.rearrange("r f o -> f r o")),
                (b_rel_sb[:, :], b_rel.rearrange("r o -> (r o)").partition_broadcast(P)),
            ] + [(bn2_rep[:, t * D:(t + 1) * D], bn2.partition_broadcast(P)) for t in range(TC)]
            in_zeros = [
                (bias_node[:, H1:2 * H1], be1.partition_broadcast(P)),
                (bias_node[:, 2 * H1:P], bn1.partition_broadcast(P)),
            ] + [
                (w1_pair[b * EA:(b + 1) * EA, q, (2 * q + b) * H1:(2 * q + b + 1) * H1], we1[2 * D:2 * D + EA, :])
                for q in range(2) for b in range(2)
            ] + [(w2_tile[j * H1:(j + 1) * H1, j, :], we2) for j in range(TC)] \
              + [(wn2_half[a * H2:(a + 1) * H2, a, :], wn2) for a in range(2)]
            assert len(plain) + len(in_zeros) == N_CONST
            for there, source in plain:
                sp.dma_start(there, source).then_inc(consts_landed, 16)
            sp.wait_ge(zeroed, 4)
            for there, source in in_zeros:
                sp.dma_start(there, source).then_inc(consts_landed, 16)

            sp.wait_ge(range_set, 3)
            sp.dma_start(base_d, least[:, :]).then_inc(range_stored, 16)
            sp.dma_start(range_d, most[:, :]).then_inc(range_stored, 16)
            sp.wait_ge(range_stored, 32)
            sp.dma_start(range_row[0:1, :], range_d.rearrange("q k -> (q k)").partition_broadcast(1)).then_inc(range_back, 16)
            sp.dma_start(base0[:, :], base_d.rearrange("q k -> (q k)").partition_broadcast(P)).then_inc(range_back, 16)
            sp.wait_ge(rowid_set, 1)
            sp.dma_start(row_tab, rel_f[:, :].bitcast(i32)).then_inc(rowid_stored, 16)

            def load_x(g, b):
                sp.dma_start(x_in[:, b, :, :], node_rows(x, g)).then_inc(x_landed[b], 16)

            def store_tables(g):
                sp.wait_ge(pqr_biased, 2 * g + 2)
                hold(sp)
                sp.wait_ge(lo_done, g + 1)
                hold(sp)
                sp.dma_start(node_rows(p_tab, g), pqr[:, :, 0:H1]).then_inc(tables_stored, 16)
                for t, part in zip(qr_tab, (qr_hi, qr_mid, qr_lo)):
                    sp.dma_start(node_rows(t, g), part[:, :, :]).then_inc(tables_stored, 16)

            load_x(0, 0)
            load_x(1, 1)
            with sp.Fori(0, NG // 2 - 1) as it:
                for b in range(2):
                    g = it * 2 + b
                    store_tables(g)
                    sp.wait_ge(res_done, g + 1)
                    hold(sp)
                    load_x(g + 2, b)
            for g in (NG - 2, NG - 1):
                store_tables(g)
            sp.wait_ge(tables_stored, 64 * NG)

            passes = number_of_passes(sp)

            def layer0_pass(m):
                sp.wait_ge(pass_ready, m + 1)
                hold(sp)

                def step(c):
                    s = c.slot
                    sp.wait_ge(prow_landed[s], c.turn * (16 * TC))
                    hold(sp)
                    sp.dma_start(idx[s][:, :], src_t[:, ds(c.i * TC, TC)]).then_inc(idx_landed[s], 16)
                    sp.wait_ge(h1_summed[s], c.turn)
                    hold(sp)
                    sp.dma_start(ea[s][:, :], edge_cols[ds(c.i, 1), :, :].rearrange("c p n -> (c p) n")).then_inc(ea_landed[s], 16)
                    sp.wait_ge(hot_built[s], c.turn)
                    hold(sp)
                    sp.dma_start(dst_wide[s], dst_c[ds(c.i, 1), :].rearrange("c e -> (c e)").partition_broadcast(3 * W))\
                      .then_inc(dst_wide_landed[s], 16)
                    start = window_start(sp, c)
                    sp.wait_ge(h2_summed[s], c.turn)
                    hold(sp)
                    for k in range(3):
                        sp.dma_start(qr_w[s][k * W:(k + 1) * W, :], qr_tab[k][ds(start, W), :]).then_inc(qr_landed[s], 16)

                all_chunks(sp, m, step)

            with sp.Fori(0, passes) as m:
                layer0_pass(m)

            with sp.Fori(0, NTILE // 2) as it:
                for b in range(2):
                    sp.wait_ge(rel_biased[b], 2 * it + 2)
                    hold(sp)
                    sp.dma_start(rel_tab[ds((it * 2 + b) * (P * R), P * R), :].rearrange("(p r) o -> p (r o)", r=R),
                                 rel_rows[:, b, :]).then_inc(rel_stored[b], 16)
            for b in range(2):
                sp.wait_ge(rel_stored[b], 16 * (NTILE // 2))
            sp.wait_ge(rowid_stored, 16)

            passes = number_of_passes(sp)

            def layer1_pass(m):
                def step(c):
                    s = c.slot
                    sp.wait_ge(rows_landed[s], c.turn * (16 * TC))
                    hold(sp)
                    sp.dma_start(idx[s][:, :], row_tab[:, ds(c.i * TC, TC)]).then_inc(idx1_landed[s], 16)

                all_chunks(sp, m, step)

            sp.wait_ge(agg_cleared, 1)
            with sp.Fori(0, passes) as m:
                layer1_pass(m)

            with sp.Fori(0, NG // 2) as it:
                for b in range(2):
                    g = it * 2 + b
                    sp.wait_ge(fin_added, g + 1)
                    hold(sp)
                    sp.dma_start(node_rows(out, g), x_in[:, b, :, :]).then_inc(out_stored[b], 16)
            for b in range(2):
                sp.wait_ge(out_stored[b], 16 * (NG // 2))

        @block.gpsimd
        def _(pool):
            pool.memset(bias_node[:, 0:H1], 0.0).then_inc(zeroed, 1)
            pool.memset(w1_pair[:, :, :], 0.0).then_inc(zeroed, 1)
            pool.memset(w2_tile[:, :, :], 0.0).then_inc(zeroed, 1)
            pool.memset(wn2_half[:, :, :], 0.0).then_inc(zeroed, 1)
            pool.iota(iota_i[:, :], [[1, W]], base=0, channel_multiplier=0).then_inc(ramps_set, 1)
            for k in range(3):
                pool.wait_ge(ramps_set, k + 1)
                pool.iota(row_i[k * W:(k + 1) * W, :], [[0, 1]], base=0, channel_multiplier=1).then_inc(ramps_set, 1)
            pool.wait_ge(ramps_set, 4)
            pool.memset(ident[:, :], 0.0).then_inc(ident_set, 1)
            pool.wait_ge(ident_set, 1)
            pool.affine_select(out=ident[:, :], in_=ident[:, :], compare_op=ALU.not_equal, fill=1.0, base=0,
                               pattern=[[-1, P]], channel_multiplier=1).then_inc(ident_set, 1)
            pool.iota(pass_i[:, :], [[W, MAXPASS]], base=0, channel_multiplier=0).then_inc(ramps_set, 1)

            def gather(c, table, rows_of, used, idx_there, landed):
                s = c.slot
                pool.wait_ge(used[s], c.turn)
                hold(pool)
                pool.wait_ge(idx_there[s], 16 * c.turn + 16)
                hold(pool)
                for t in range(TC):
                    pool.indirect_dma_start(
                        out=rows_of[s][:, t, :], out_offset=None, in_=table,
                        in_offset=bass.IndirectOffsetOnAxis(ap=idx[s][:, t:t + 1], axis=0),
                    ).then_inc(landed[s], 16)

            pool.wait_ge(tables_stored, 64 * NG)
            passes = number_of_passes(pool)
            with pool.Fori(0, passes) as m:
                all_chunks(pool, m, lambda c: gather(c, p_tab, prow, h1_summed, idx_landed, prow_landed))

            for b in range(2):
                pool.wait_ge(rel_stored[b], 16 * (NTILE // 2))
            passes = number_of_passes(pool)
            with pool.Fori(0, passes) as m:
                all_chunks(pool, m, lambda c: gather(c, rel_tab, rows, rows_summed, idx1_landed, rows_landed))

        @block.scalar
        def _(act):
            def std_and_hT(k):
                act.wait_ge(eps_added, k + 1)
                act.activation(std[:, :], var_eps[:, :], ACT.Sqrt).then_inc(std_done, 1)
                act.wait_ge(h_transposed, 2 * k + 1)
                act.activation(hT[:, 0:4 * P], bank[0][:, 0:4 * P], ACT.Copy).then_inc(hT_copied, 1)
                act.wait_ge(h_transposed, 2 * k + 2)
                act.activation(hT[:, 4 * P:TPG * P], bank[1][:, 0:(TPG - 4) * P], ACT.Copy).then_inc(hT_copied, 1)

            with act.Fori(0, NG) as g:
                std_and_hT(g)
                act.wait_ge(pqr_biased, 2 * g + 2)
                act.wait_ge(tables_stored, 64 * g)
                act.activation(qr_hi[:, :, :], pqr[:, :, H1:P], ACT.Copy).then_inc(hi_done, 1)
                act.wait_ge(res1_done, g + 1)
                act.activation(qr_mid[:, :, :], qr_res[:, :, :], ACT.Copy).then_inc(mid_done, 1)

            def relu_h2(c):
                act.wait_ge(h2_summed[c.slot], c.turn + 1)
                act.activation(h2_sb[:, :], ps_h2[:, 0:2 * P], ACT.Relu).then_inc(h2_done, 1)

            def copy_tile_sums(c):
                act.wait_ge(tiles_summed, c.n + 1)
                act.activation(tile_sums[:, :], ps_tiles[:, 0:D], ACT.Copy).then_inc(tiles_copied, 1)

            def relu_msg1(c):
                act.wait_ge(msg1_summed, c.n + 1)
                act.activation(msg1_sb[:, :], ps_msg1[:, :], ACT.Relu, bias=be2_col[:, 0:1]).then_inc(msg1_done, 1)

            def relu_msg2(c):
                act.wait_ge(msg2_biased, c.n + 1)
                act.activation(msg2_sb[:, :], msg2_sb[:, :], ACT.Relu).then_inc(msg2_done, 1)

            act.wait_ge(consts_landed, 16 * N_CONST)
            passes = number_of_passes(act)

            def step(c, before, before2, after):
                if before:
                    relu_h2(before)
                if before2:
                    copy_tile_sums(before2)
                if c:
                    relu_msg1(c)
                if before:
                    relu_msg2(before)

            with act.Fori(0, passes) as m:
                pipelined(m, act, step)

            def stage_agg(k, g):
                act.wait_ge(agg_transposed, 2 * k)
                act.activation(agg_group[:, :], agg[:, ds(g * (TPG * P), TPG * P)], ACT.Copy).then_inc(agg_staged, 1)

            act.wait_ge(agg_added, passes * NCH + 1)
            with act.Fori(0, NG) as g:
                stage_agg(g, g)
                std_and_hT(g + NG)

            for b in range(2):
                act.wait_ge(agg1_added[b], passes * (NCH // 2))
            with act.Fori(0, NG // 2) as it:
                for b in range(2):
                    g = it * 2 + b
                    stage_agg(g + NG, g)
                    act.wait_ge(out_stored[b], 16 * it)
                    for a, (t0, t1) in enumerate(((0, 4), (4, TPG))):
                        act.wait_ge(agg_transposed, 2 * (g + NG) + a + 1)
                        act.activation(x_in[:, b, t0:t1, :],
                                       bank[2 + a][:, 0:(t1 - t0) * P].rearrange("p (j d) -> p j d", d=D), ACT.Relu)\
                           .then_inc(fin_relu, 1)

        @block.vector
        def _(dve):
            dve.wait_ge(dst_landed, 16)
            dve.tensor_reduce(least[:, :], dst_rows[:, :, :].bitcast(u32), AX.X, ALU.min).then_inc(range_set, 1)
            dve.tensor_reduce(most[:, :], dst_rows[:, :, :], AX.X, ALU.max).then_inc(range_set, 1)
            dve.wait_ge(range_set, 2)
            dve.tensor_tensor(most[:, :], most[:, :], least[:, :], ALU.subtract).then_inc(range_set, 1)
            dve.wait_ge(ids_landed, 32)
            dve.scalar_tensor_tensor(out=rel_f[:, :].bitcast(i32), in0=rel_f[:, :].bitcast(i32), scalar=float(R),
                                     in1=etype_i, op0=ALU.mult, op1=ALU.add).then_inc(rowid_set, 1)
            dve.wait_ge(dstf_landed, 16)
            dve.tensor_copy(dst_f[:, :], dst_f[:, :].bitcast(i32)).then_inc(prep_step, 1)
            dve.wait_ge(ramps_set, 5)
            dve.tensor_copy(iota_f[:, :], iota_i[:, :]).then_inc(prep_step, 1)
            dve.tensor_copy(row_f[:, :], row_i[:, :])
            dve.tensor_copy(pass_f[:, :], pass_i[:, :]).then_inc(prep_step, 1)
            dve.wait_ge(ident_set, 2)
            dve.tensor_tensor(fold_tiles[:, :], ident[:, 0:W], ident[:, W:2 * W], ALU.add).then_inc(fold_step, 1)
            for t in range(2, TC):
                dve.wait_ge(fold_step, t - 1)
                dve.tensor_tensor(fold_tiles[:, :], fold_tiles[:, :], ident[:, t * W:(t + 1) * W], ALU.add).then_inc(fold_step, 1)
            dve.wait_ge(consts_landed, 16 * N_CONST)
            dve.wait_ge(range_back, 32)
            dve.tensor_reduce(range_max[:, :], range_row[:, :], AX.X, ALU.max).then_inc(prep_step, 1)
            dve.tensor_scalar_add(base0[:, :], base0[:, :], -float(W)).then_inc(prep_step, 1)
            dve.wait_ge(prep_step, 5)
            dve.tensor_scalar(pass_f[:, :], pass_f[:, :], range_max[0:1, 0:1], None, ALU.is_le).then_inc(prep_step, 1)
            dve.wait_ge(prep_step, 6)
            dve.tensor_reduce(passes_f[:, :], pass_f[:, :], AX.X, ALU.add).then_inc(prep_step, 1)
            dve.wait_ge(prep_step, 7)
            dve.tensor_copy(passes_i[:, :], passes_f[:, :]).then_inc(passes_set, 1)

            def layer_norm(k, source):
                for j in range(TPG):
                    ins = dve.bn_stats(stats[:, j, :], source(j))
                ins.then_inc(stats_done, 1)
                dve.wait_ge(stats_done, k + 1)
                hold(dve)
                for j in range(TPG):
                    ins = dve.bn_aggr(mv[:, j, :], stats[:, j, :])
                ins.then_inc(aggr_done, 1)
                dve.wait_ge(aggr_done, k + 1)
                dve.tensor_scalar_add(var_eps[:, :], mv[:, :, 1], EPS).then_inc(eps_added, 1)
                dve.wait_ge(h_transposed, 2 * k)
                dve.tensor_tensor(h[:, :, :], source(None), wide(mv[:, :, 0], D), ALU.subtract).then_inc(centred, 1)
                dve.wait_ge(std_done, k + 1)
                dve.reciprocal(rstd[:, :], std[:, :]).then_inc(rstd_done, 1)
                dve.wait_ge(rstd_done, k + 1)
                dve.wait_ge(centred, k + 1)
                dve.scalar_tensor_tensor(out=h[:, :, :], in0=h[:, :, :], scalar=0.0, in1=wide(rstd[:, :], D),
                                         op0=ALU.max, op1=ALU.mult).then_inc(h_done, 1)

            with dve.Fori(0, NG // 2) as it:
                for b in range(2):
                    g = it * 2 + b
                    dve.wait_ge(x_landed[b], 16 * it + 16)
                    layer_norm(g, lambda j: x_in[:, b, :, :] if j is None else x_in[:, b, j, :])
                    dve.wait_ge(h_done, g + 1)
                    dve.tensor_tensor(res[:, ds(g * TPG, TPG), :], h[:, :, :], x_in[:, b, :, :], ALU.add)\
                       .then_inc(res_done, 1)
                    dve.wait_ge(tables_stored, 64 * g)
                    for a, (t0, t1) in enumerate(((0, 4), (4, TPG))):
                        dve.wait_ge(pqr_ready, 2 * g + a + 1)
                        dve.tensor_tensor(pqr[:, t0:t1, :],
                                          bank[2 + a][:, 0:(t1 - t0) * P].rearrange("p (j d) -> p j d", d=P),
                                          tiled(bias_node[:, :], t1 - t0), ALU.add).then_inc(pqr_biased, 1)
                    dve.wait_ge(hi_done, g + 1)
                    dve.tensor_tensor(qr_res[:, :, :], pqr[:, :, H1:P], qr_hi[:, :, :], ALU.subtract).then_inc(res1_done, 1)
                    dve.wait_ge(mid_done, g + 1)
                    dve.tensor_tensor(qr_lo[:, :, :], qr_res[:, :, :], qr_mid[:, :, :], ALU.subtract).then_inc(lo_done, 1)

            def set_windows(m, step, ready):
                dve.tensor_scalar_add(base_f[:, :], base_f[:, :], float(W)).then_inc(step, 1)
                dve.wait_ge(step, 2 * m + 1)
                dve.tensor_scalar_min(base_c[:, :], base_f[:, :], float(TOP)).then_inc(step, 1)
                dve.wait_ge(step, 2 * m + 2)
                dve.tensor_copy(base_i[:, :], base_c[:, :])
                dve.tensor_tensor(rel_f[:, :].rearrange("p (c t) -> p c t", t=TC), dst_f[:, :].rearrange("p (c t) -> p c t", t=TC),
                                  wide(base_c[:, :], TC), ALU.subtract).then_inc(ready, 1)

            dve.wait_ge(rowid_stored, 16)
            dve.memset(agg[:, :], 0.0).then_inc(agg_added, 1)
            dve.tensor_copy(base_f[:, :], base0[:, :]).then_inc(prep_step, 1)
            dve.wait_ge(prep_step, 8)
            passes = number_of_passes(dve)

            def build_hot(c):
                s = c.slot
                offset = rel_f[:, ds(c.i * TC, TC)]
                dve.tensor_tensor(hot[s][:, :, :], tiled(iota_f[:, 0:W], TC), wide(offset, W), ALU.is_equal)
                dve.wait_ge(dst_wide_landed[s], 16 * c.turn + 16)
                hold(dve)
                dve.tensor_scalar(hotT[s % 2][:, :], dst_wide[s], base_c[0:3 * W, ds(c.i, 1)], row_f[:, 0:1],
                                  ALU.subtract, ALU.is_equal).then_inc(hot_built[s], 1)

            def relu_h1(c):
                dve.wait_ge(h1_summed[c.slot], c.turn + 1)
                dve.tensor_scalar_max(h1_sb[:, :], ps_h1[:, 0:P], 0.0).then_inc(h1_done, 1)

            def add_chunk(c):
                start = window_start(dve, c)
                dve.wait_ge(chunk_summed, c.n + 1)
                dve.wait_ge(agg_added, c.n + 1)
                dve.tensor_tensor(agg[:, ds(start, W)], agg[:, ds(start, W)], ps_agg[:, 0:W], ALU.add).then_inc(agg_added, 1)

            def bias_msg2(c):
                dve.wait_ge(msg2_summed, c.n + 1)
                dve.tensor_tensor(msg2_sb[:, :], ps_msg2[:, :], bn2_rep[:, :], ALU.add).then_inc(msg2_biased, 1)

            def step(c, before, before2, after):
                if c:
                    relu_h1(c)
                if after:
                    build_hot(after)
                if before2:
                    add_chunk(before2)
                if before:
                    bias_msg2(before)

            with dve.Fori(0, passes) as m:
                dve.wait_ge(chunk_summed, m * NCH)
                set_windows(m, pass_step, pass_ready)
                dve.wait_ge(pass_ready, m + 1)
                hold(dve)
                build_hot(Chunk(m, 0, 0))
                pipelined(m, dve, step)

            with dve.Fori(0, NG // 2) as it:
                for b in range(2):
                    g = it * 2 + b
                    for a, (t0, t1) in enumerate(((0, 4), (4, TPG))):
                        there = res[:, ds(g * TPG + t0, t1 - t0), :]
                        dve.wait_ge(agg_transposed, 2 * g + a + 1)
                        dve.tensor_tensor(there, there, bank[2 + a][:, 0:(t1 - t0) * P].rearrange("p (j d) -> p j d", d=D),
                                          ALU.add).then_inc(mid_added, 1)
                    dve.wait_ge(mid_added, 2 * g + 2)
                    hold(dve)
                    layer_norm(g + NG, lambda j: res[:, ds(g * TPG, TPG), :] if j is None else
                               res[:, ds(g * TPG + j, 1), :].rearrange("p j d -> p (j d)"))
                    for j in range(TPG):
                        buf, turn = rel_buffer(it, b, j)
                        dve.wait_ge(rel_stored[buf], 16 * turn)
                        for a in range(2):
                            dve.wait_ge(rel_ready[buf], 2 * turn + a + 1)
                            cols = slice(a * 512, a * 512 + 512)
                            dve.tensor_tensor(rel_rows[:, buf, cols], bank[4 + 2 * buf + a][:, :], b_rel_sb[:, cols], ALU.add)\
                               .then_inc(rel_biased[buf], 1)

            dve.wait_ge(agg_staged, NG)
            dve.memset(agg[:, :], 0.0).then_inc(agg_cleared, 1)
            dve.wait_ge(agg_cleared, 1)
            dve.wait_ge(weight_landed, 16)
            dve.tensor_copy(base_f[:, :], base0[:, :]).then_inc(prep_step, 1)
            dve.wait_ge(prep_step, 9)

            with dve.Fori(0, passes) as m:
                for s in range(SL):
                    dve.wait_ge(rows_summed[s], m * (NCH // SL))
                set_windows(m, pass1_step, pass1_ready)
                dve.wait_ge(pass1_ready, m + 1)
                hold(dve)

                def step(c):
                    s = c.slot
                    dve.wait_ge(rows_summed[s], c.turn)
                    for t in range(TC):
                        at = ds(c.i * TC + t, 1)
                        ins = dve.tensor_scalar(hot[s][:, t, :], iota_f[:, 0:W], rel_f[:, at], w_f[:, at],
                                                ALU.is_equal, ALU.mult)
                    ins.then_inc(hot1_built, 1)
                    start = window_start(dve, c)
                    dve.wait_ge(rows_summed[s], c.turn + 1)
                    dve.wait_ge(agg1_added[1 - s % 2], 2 * c.turn + (s + 1) // 2)
                    dve.tensor_tensor(agg[:, ds(start, W)], agg[:, ds(start, W)], bank[6 + s % 2][:, 0:W], ALU.add)\
                       .then_inc(agg1_added[s % 2], 1)

                all_chunks(dve, m, step)

            with dve.Fori(0, NG // 2) as it:
                for b in range(2):
                    g = it * 2 + b
                    dve.wait_ge(fin_relu, 2 * g + 2)
                    dve.tensor_tensor(x_in[:, b, :, :], x_in[:, b, :, :], res[:, ds(g * TPG, TPG), :], ALU.add)\
                       .then_inc(fin_added, 1)

        @block.tensor
        def _(pe):
            pe.wait_ge(ident_set, 2)
            pe.wait_ge(consts_landed, 16 * N_CONST)
            pe.wait_ge(fold_step, TC - 1)
            HALVES = ((0, 4), (4, TPG))

            def transpose_h(k):
                pe.wait_ge(h_done, k + 1)
                pe.wait_ge(hT_copied, 2 * k)
                for a, (t0, t1) in enumerate(HALVES):
                    for j in range(t0, t1):
                        ins = pe.transpose(bank[a][:, (j - t0) * P:(j - t0 + 1) * P], h[:, j, :], ident[:, :])
                    ins.then_inc(h_transposed, 1)

            def transpose_agg(k, free):
                pe.wait_ge(agg_staged, k + 1)
                free()
                for a, (t0, t1) in enumerate(HALVES):
                    for j in range(t0, t1):
                        ins = pe.transpose(bank[2 + a][:, (j - t0) * P:(j - t0 + 1) * P],
                                           agg_group[:, j * P:(j + 1) * P], ident[:, :])
                    ins.then_inc(agg_transposed, 1)

            with pe.Fori(0, NG) as g:
                transpose_h(g)
                pe.wait_ge(pqr_biased, 2 * g)
                for a, (t0, t1) in enumerate(HALVES):
                    pe.wait_ge(hT_copied, 2 * g + a + 1)
                    for j in range(t0, t1):
                        ins = pe.matmul(bank[2 + a][:, (j - t0) * P:(j - t0 + 1) * P],
                                        hT[:, j * P:(j + 1) * P], w_node[:, :], start=True, stop=True)
                    ins.then_inc(pqr_ready, 1)

            def sum_h1(c):
                s = c.slot
                pe.wait_ge(ea_landed[s], 16 * c.turn + 16)
                for q in range(2):
                    pe.matmul(ps_h1[:, 0:P], w1_pair[:, q, :], ea[s][:, q * P:(q + 1) * P], start=(q == 0), stop=False)
                pe.wait_ge(qr_landed[s], 48 * c.turn + 48)
                pe.wait_ge(hot_built[s], c.turn + 1)
                for t in range(TC):
                    pe.matmul(ps_h1[t * H1:(t + 1) * H1, 0:P], qr_w[s][:, 0:H1], hotT[s % 2][:, t * P:(t + 1) * P],
                              start=False, stop=False)
                pe.wait_ge(prow_landed[s], 16 * TC * c.turn + 16 * TC)
                pe.matmul(ps_h1[:, 0:P], prow[s][:, :, :].rearrange("p t o -> p (t o)"), ident[:, :], start=False, stop=True)\
                  .then_inc(h1_summed[s], 1)

            def sum_msg1(c):
                pe.wait_ge(h1_done, c.n + 1)
                for t in range(TC):
                    ins = pe.matmul(ps_msg1[:, t * P:(t + 1) * P], w2_tile[:, t, :], h1_sb[:, :], start=True, stop=True)
                ins.then_inc(msg1_summed, 1)

            def sum_h2(c):
                s = c.slot
                pe.wait_ge(msg1_done, c.n + 1)
                for a in range(2):
                    there = ps_h2[a * H2:(a + 1) * H2, 0:2 * P]
                    cols = slice(a * 2 * P, (a + 1) * 2 * P)
                    pe.matmul(there, wn1_msg[:, :], msg1_sb[:, cols], start=True, stop=False)
                    ins = pe.matmul(there, qr_w[s][:, H1:QR], hotT[s % 2][:, cols], start=False, stop=True)
                ins.then_inc(h2_summed[s], 1)

            def sum_msg2(c):
                pe.wait_ge(h2_done, c.n + 1)
                for t in range(TC):
                    a, b = t // 2, t % 2
                    ins = pe.matmul(ps_msg2[:, t * P:(t + 1) * P], h2_sb[:, b * P:(b + 1) * P], wn2_half[:, a, :],
                                    start=True, stop=True)
                ins.then_inc(msg2_summed, 1)

            def sum_tiles(c):
                pe.wait_ge(msg2_done, c.n + 1)
                for t in range(TC):
                    ins = pe.matmul(ps_tiles[t * W:(t + 1) * W, 0:D], hot[c.slot][:, t, :], msg2_sb[:, t * P:(t + 1) * P],
                                    start=True, stop=True)
                ins.then_inc(tiles_summed, 1)

            def sum_chunk(c):
                pe.wait_ge(tiles_copied, c.n + 1)
                pe.wait_ge(agg_added, c.n + 1)
                pe.matmul(ps_agg[:, 0:W], tile_sums[:, :], fold_tiles[:, :], start=True, stop=True).then_inc(chunk_summed, 1)

            passes = number_of_passes(pe)

            def step(c, before, before2, after):
                if before:
                    sum_h2(before)
                if c:
                    sum_h1(c)
                if before2:
                    sum_tiles(before2)
                if c:
                    sum_msg1(c)
                if before2:
                    sum_chunk(before2)
                if before:
                    sum_msg2(before)

            with pe.Fori(0, passes) as m:
                pipelined(m, pe, step)

            with pe.Fori(0, NG // 2) as it:
                for b in range(2):
                    g = it * 2 + b
                    transpose_agg(g, lambda: pe.wait_ge(mid_added, 2 * g))
                    transpose_h(g + NG)
                    pe.wait_ge(hT_copied, 2 * (g + NG) + 2)
                    for j in range(TPG):
                        buf, turn = rel_buffer(it, b, j)
                        pe.wait_ge(rel_biased[buf], 2 * turn)
                        for a in range(2):
                            pe.matmul(bank[4 + 2 * buf + a][:, :], hT[:, j * P:(j + 1) * P],
                                      w_rel_sb[:, a * R // 2:(a + 1) * R // 2, :].rearrange("f r o -> f (r o)"),
                                      start=True, stop=True).then_inc(rel_ready[buf], 1)

            def step1(c):
                s = c.slot
                pe.wait_ge(hot1_built, c.n + 1)
                pe.wait_ge(rows_landed[s], 16 * TC * c.turn + 16 * TC)
                pe.wait_ge(agg1_added[s % 2], 2 * c.turn + s // 2)
                for t in range(TC):
                    ins = pe.matmul(bank[6 + s % 2][:, 0:W], rows[s][:, t, :], hot[s][:, t, :],
                                    start=(t == 0), stop=(t == TC - 1))
                ins.then_inc(rows_summed[s], 1)

            with pe.Fori(0, passes) as m:
                all_chunks(pe, m, step1)

            with pe.Fori(0, NG) as g:
                transpose_agg(g + NG, lambda: pe.wait_ge(fin_relu, 2 * g))

    return nc


def kernel(x, src, dst, edge_attr_64, edge_type_8, edge_weight1, L0_gnn_We1, L0_gnn_be1, L0_gnn_We2, L0_gnn_be2,
           L0_gnn_Wn1, L0_gnn_bn1, L0_gnn_Wn2, L0_gnn_bn2, L1_gnn_W, L1_gnn_b):
    import numpy as np
    import concourse.bacc as bacc
    from concourse import mybir
    from concourse.bass_utils import run_bass_kernel_spmd

    nodes, width = x.shape
    edges = src.shape[0]
    group, chunk, tiles, block = 2 * 7 * 128, 512, 4, 4 * 512
    n_pad = -(-nodes // group) * group - nodes
    e_pad = -(-edges // block) * block - edges
    n_chunks = (edges + e_pad) // chunk

    def padded(a, n, value=0):
        a = np.asarray(a)
        return np.concatenate([a, np.full((n,) + a.shape[1:], value, a.dtype)])

    def by_partition(a):
        return np.ascontiguousarray(a.reshape(n_chunks, chunk // tiles, tiles).transpose(1, 0, 2).reshape(chunk // tiles, -1))

    def tile_major(a):
        return a.reshape(n_chunks, chunk // tiles, tiles).transpose(0, 2, 1).reshape(n_chunks, chunk)

    def edge_columns(a):
        a = a.reshape(n_chunks, chunk // tiles, 2, 2, a.shape[1])
        return a.transpose(0, 3, 4, 2, 1).reshape(n_chunks, 2 * a.shape[-1], 2 * chunk // tiles)

    dst_pad = padded(dst, e_pad, -1)
    arrays = {
        "x": padded(x, n_pad),
        "src_t": by_partition(padded(src, e_pad)),
        "dst_t": by_partition(dst_pad),
        "etype_t": by_partition(padded(edge_type_8, e_pad)),
        "weight_t": by_partition(padded(np.asarray(edge_weight1)[:, 0], e_pad)),
        "dst_c": tile_major(dst_pad),
        "edge_cols": edge_columns(padded(edge_attr_64, e_pad)),
        "we1": L0_gnn_We1, "be1": L0_gnn_be1, "we2": L0_gnn_We2, "be2": L0_gnn_be2,
        "wn1": L0_gnn_Wn1, "bn1": L0_gnn_bn1, "wn2": L0_gnn_Wn2, "bn2": L0_gnn_bn2,
        "w_rel": L1_gnn_W, "b_rel": L1_gnn_b,
    }
    arrays = {f"in_{k}": np.ascontiguousarray(a) for k, a in arrays.items()}
    nc = bacc.Bacc("TRN2", target_bir_lowering=False, num_devices=1)
    args = [nc.dram_tensor(k, a.shape, mybir.dt.from_np(a.dtype), kind="ExternalInput").ap() for k, a in arrays.items()]
    args.append(nc.dram_tensor("out_x", [nodes + n_pad, width], mybir.dt.float32, kind="ExternalOutput").ap())
    gnn_two_layers(nc, *args)
    got = run_bass_kernel_spmd(nc, [arrays], core_ids=[0])
    return got.results[0]["out_x"][:nodes]
```

```python
import concourse.bass as bass
from concourse import mybir
from contextlib import ExitStack


def gnn_two_layers(nc, x, src_t, dst_t, etype_t, weight_t, dst_c, edge_cols,
                   we1, be1, we2, be2, wn1, bn1, wn2, bn2, w_rel, b_rel, out):
    f32, bf16, i32, u32 = mybir.dt.float32, mybir.dt.bfloat16, mybir.dt.int32, mybir.dt.uint32
    ALU, ACT, AX = mybir.AluOpType, mybir.ActivationFunctionType, mybir.AxisListType
    ds = bass.ds

    P = 128
    NPAD, D = x.shape
    TPG = 7
    NG = NPAD // (P * TPG)
    NTILE = NG * TPG
    TC = 4
    CH = TC * P
    NCH = src_t.shape[1] // TC
    NROW = dst_c.shape[0]
    NPAIR = NCH // 2
    SL = 4
    W = 32
    EA = edge_cols.shape[1] // 2
    H1 = we2.shape[0]
    H2 = wn2.shape[0]
    QR = H1 + H2
    R = w_rel.shape[0]
    MAXPASS = (NPAD + W - 1) // W
    TOP = NPAD - W
    KEY = W + 2
    EPS = 1e-5
    assert NG % 2 == 0 and NCH % 2 == 0 and NCH > 2 * SL and TC * H1 == P and 2 * H2 == P and 2 * EA == P and 3 * W <= P
    QP = max(q for q in range(1, P + 1) if NROW % q == 0)
    QC = NROW // QP

    p_tab = nc.dram_tensor("p_tab", [NPAD, H1], f32).ap()
    qr_tab = nc.dram_tensor("qr_tab", [3, NPAD, QR], bf16).ap()
    h_tab = nc.dram_tensor("h_tab", [NPAD, D], f32).ap()
    base_d = nc.dram_tensor("base_d", [QP, QC], f32).ap()
    range_d = nc.dram_tensor("range_d", [QP, QC], f32).ap()

    ctx = ExitStack()
    with ctx:
        def sb(name, shape, dt=f32):
            return ctx.enter_context(nc.sbuf_tensor(name, shape, dt))

        def sem(name):
            return ctx.enter_context(nc.semaphore(name))

        def slot_sems(name, n=SL):
            return [sem(f"{name}{k}") for k in range(n)]

        w_node = sb("w_node", [P, P])
        bias_node = sb("bias_node", [P, P])
        w1_pair = sb("w1_pair", [P, 2, P])
        w2_tile = sb("w2_tile", [P, TC, P])
        wn1_msg = sb("wn1_msg", [P, H2])
        wn2_half = sb("wn2_half", [P, 2, P])
        be2_col = sb("be2_col", [P, 1])
        bn2_rep = sb("bn2_rep", [P, TC * D])
        w_rel_sb = sb("w_rel_sb", [P, R, D])
        b_rel_sb = sb("b_rel_sb", [R, D])
        ident = sb("ident", [P, P])
        fold_tiles = sb("fold_tiles", [P, W])
        iota_i = sb("iota_i", [P, W], i32)
        iota_f = sb("iota_f", [P, W])
        iota_key_i = sb("iota_key_i", [P, R, W], i32)
        iota_key = sb("iota_key", [P, R, W])
        row_i = sb("row_i", [3 * W, 1], i32)
        row_f = sb("row_f", [3 * W, 1])

        dst_f = sb("dst_f", [P, NCH * TC])
        et_key = sb("et_key", [P, NCH * TC])
        w_f = sb("w_f", [P, NCH * TC])
        least = sb("least", [QP, QC])
        most = sb("most", [QP, QC])
        base0 = sb("base0", [P, NROW])
        base_f = sb("base_f", [P, NROW])
        base_c = sb("base_c", [P, NROW])
        base_i = sb("base_i", [P, NROW], i32)
        range_max = sb("range_max", [1, 1])
        passes_f = sb("passes_f", [1, 1])
        passes_i = sb("passes_i", [1, 1], i32)

        res = sb("res", [P, NTILE, D])
        agg = sb("agg", [P, NPAD])
        taken = 0

        def in_agg(n, parts=P):
            nonlocal taken
            taken += n
            assert taken <= NPAD
            return agg[0:parts, taken - n:taken]

        dst_rows = in_agg(QC * CH, QP).bitcast(i32).rearrange("q (k e) -> q k e", e=CH)
        range_row = in_agg(NROW, 1)
        pass_i = in_agg(MAXPASS, 1).bitcast(i32)
        pass_f = in_agg(MAXPASS, 1)
        x_in = sb("x_in", [P, 2, TPG, D])
        hT = sb("hT", [P, TPG * P])
        stats = sb("stats", [P, 2, TPG, 6])
        mv = sb("mv", [P, 2, TPG, 2])
        var_eps = sb("var_eps", [P, 2, TPG])
        std = sb("std", [P, 2, TPG])
        rstd = sb("rstd", [P, 2, TPG])
        agg_group = [sb("agg_group", [P, TPG * P]), hT]
        h = [x.rearrange("p (j d) -> p j d", d=D) for x in (sb("h", [P, TPG * P])[:, :], agg_group[0][:, :])]
        TABLES = TPG * (P + QR) + 3 * TPG * QR // 2
        shared = sb("shared", [P, max(TABLES, SL * TC * (EA + H1) + 2 * CH)])
        taken_by = {"tables": 0, "edges": 0}

        def in_shared(who, n):
            taken_by[who] += n
            return shared[:, taken_by[who] - n:taken_by[who]]

        tables_from = taken
        table_places = [in_shared("tables", TABLES), in_agg(TABLES)]

        def table_rows(first, n, dt=f32):
            bits = 2 if dt == bf16 else 1
            return [place[:, TPG * first:TPG * first + TPG * n // bits].bitcast(dt).rearrange("p (j d) -> p j d", d=n)
                    for place in table_places]

        pqr = table_rows(0, P)
        qr_res = table_rows(P, QR)
        qr_hi, qr_mid, qr_lo = (table_rows(P + QR + k * QR // 2, QR, bf16) for k in range(3))
        ea = [in_shared("edges", TC * EA) for s in range(SL)]
        prow = [in_shared("edges", TC * H1).rearrange("p (t o) -> p t o", o=H1) for s in range(SL)]
        msg1_sb, msg2_sb = (in_shared("edges", CH) for _ in range(2))
        rows_place = sb("rows_place", [P, SL * TC * D])
        dst_wide = [rows_place[0:3 * W, s * CH:(s + 1) * CH].bitcast(i32) for s in range(SL)]
        rows = [rows_place[:, s * TC * D:(s + 1) * TC * D].rearrange("p (t d) -> p t d", d=D) for s in range(SL)]

        RW = R * W
        hot_rel = [shared[:, k * TC * RW:(k + 1) * TC * RW].rearrange("p (t n) -> p t n", n=RW) for k in range(2)]
        rel_sums = [x_in[:, k, :, :].rearrange("p j d -> p (j d)")[:, 0:2 * RW].rearrange("p (r c n) -> p r c n", r=R, c=2)
                    for k in range(2)]
        et_w = [sb(f"et_w{s}", [P, TC, R]) for s in range(SL)]
        w_sums = [sb(f"w_sums{k}", [R, 2, W]) for k in range(2)]
        offset = [sb(f"offset{k}", [P, 2 * TC]) for k in range(2)]
        key = [sb(f"key{k}", [P, 2 * TC]) for k in range(2)]

        idx = [sb(f"idx{s}", [P, TC], i32) for s in range(SL)]
        qr_w = [sb(f"qr_w{s}", [3 * W, QR], bf16) for s in range(SL)]
        hot = [sb(f"hot{s}", [P, TC, W]) for s in range(SL)]
        hotT = [sb(f"hotT{s}", [3 * W, CH], bf16) for s in range(2)]
        h1_sb = sb("h1_sb", [P, P])
        h2_sb = sb("h2_sb", [P, 2 * P])
        tile_sums = sb("tile_sums", [P, D])

        bank = [ctx.enter_context(nc.psum_tensor(f"bank{k}", [P, 512], f32)) for k in range(8)]
        ps_h1, ps_msg1, ps_h2, ps_msg2, ps_tiles, ps_agg = bank[0:6]

        consts_landed = sem("consts_landed")
        node_consts_landed = sem("node_consts_landed")
        dst_landed = sem("dst_landed")
        dstf_landed = sem("dstf_landed")
        zeroed = sem("zeroed")
        ident_set = sem("ident_set")
        ramps_set = sem("ramps_set")
        fold_step = sem("fold_step")
        range_set = sem("range_set")
        range_stored = sem("range_stored")
        range_back = sem("range_back")
        prep_step, edges_set = sem("prep_step"), sem("edges_set")
        ids_landed, weight_landed = sem("ids_landed"), sem("weight_landed")
        passes_set = sem("passes_set")
        x_in_moved = slot_sems("x_in_moved", 2)
        stats_done, aggr_done, eps_added = sem("stats_done"), sem("aggr_done"), sem("eps_added")
        std_done, rstd_done, centred = sem("std_done"), sem("rstd_done"), sem("centred")
        h_done, res_done = sem("h_done"), slot_sems("res_done", 2)
        h_transposed, hT_copied = slot_sems("h_transposed", 2), sem("hT_copied")
        pqr_ready, pqr_biased = sem("pqr_ready"), sem("pqr_biased")
        hi_done, res1_done, mid_done = sem("hi_done"), sem("res1_done"), sem("mid_done")
        lo_done = sem("lo_done")
        p_stored, parts_stored = slot_sems("p_stored", 2), slot_sems("parts_stored", 2)
        agg_staged, agg_transposed = slot_sems("agg_staged", 2), slot_sems("agg_transposed", 2)
        mid_added, mid_centred = slot_sems("mid_added", 2), slot_sems("mid_centred", 2)
        mid_h_done = slot_sems("mid_h_done", 2)
        agg_cleared = sem("agg_cleared")
        out_stored = sem("out_stored")
        fin_even, fin_relu, fin_odd = sem("fin_even"), sem("fin_relu"), sem("fin_odd")
        pass_ready = sem("pass_ready")
        pass_step = sem("pass_step")
        idx_landed, ea_landed = slot_sems("idx_landed"), slot_sems("ea_landed")
        qr_landed, prow_landed = slot_sems("qr_landed"), slot_sems("prow_landed")
        dst_wide_landed = slot_sems("dst_wide_landed")
        h1_summed, h2_summed, hot_built = slot_sems("h1_summed"), slot_sems("h2_summed"), slot_sems("hot_built")
        msg1_summed, msg2_summed = sem("msg1_summed"), sem("msg2_summed")
        tiles_summed, chunk_summed = sem("tiles_summed"), sem("chunk_summed")
        h1_done, msg1_done, h2_done = sem("h1_done"), sem("msg1_done"), sem("h2_done")
        msg2_biased, msg2_done = sem("msg2_biased"), sem("msg2_done")
        tiles_copied, agg_added = sem("tiles_copied"), sem("agg_added")
        idx1_landed, rows_landed = slot_sems("idx1_landed"), slot_sems("rows_landed")
        offsets_set, keys_set, hot1_built = sem("offsets_set"), sem("keys_set"), slot_sems("hot1_built")
        scattered, sums_copied = slot_sems("scattered"), slot_sems("sums_copied")
        projected, half_added, pair_added = slot_sems("projected", 2), sem("half_added"), slot_sems("pair_added", 2)
        pass1_ready, pass1_step = sem("pass1_ready"), sem("pass1_step")

        block = ctx.enter_context(nc.Block())

        w_node_parts = [
            (w_node[:, 0:H1], we1[0:D, :]),
            (w_node[:, H1:2 * H1], we1[D:2 * D, :]),
            (w_node[:, 2 * H1:P], wn1[0:D, :]),
        ]
        bias_node_parts = [
            (bias_node[:, H1:2 * H1], be1.partition_broadcast(P)),
            (bias_node[:, 2 * H1:P], bn1.partition_broadcast(P)),
        ]
        N_NODE_CONST = len(w_node_parts) + len(bias_node_parts)
        edge_consts = [
            (wn1_msg[:, :], wn1[D:2 * D, :]),
            (be2_col[:, :], be2.rearrange("(p o) -> p o", o=1)),
            (w_rel_sb[:, :, :], w_rel.rearrange("r f o -> f r o")),
            (b_rel_sb[:, :], b_rel),
        ] + [(bn2_rep[:, t * D:(t + 1) * D], bn2.partition_broadcast(P)) for t in range(TC)] + [
            (w1_pair[b * EA:(b + 1) * EA, q, (2 * q + b) * H1:(2 * q + b + 1) * H1], we1[2 * D:2 * D + EA, :])
            for q in range(2) for b in range(2)
        ] + [(w2_tile[j * H1:(j + 1) * H1, j, :], we2) for j in range(TC)] \
          + [(wn2_half[a * H2:(a + 1) * H2, a, :], wn2) for a in range(2)]
        N_CONST = len(edge_consts)

        MOVES = 16 * (NG // 2)
        HALVES = ((0, 4), (4, TPG))

        SLOT_USES = [(NCH - s + SL - 1) // SL for s in range(SL)]
        HALF_USES = [(NPAIR + 1) // 2, NPAIR // 2]

        class Chunk:

            def __init__(self, m, quad, u):
                self.m, self.slot, q = m, u % SL, quad + u // SL
                self.i = q * SL + self.slot
                self.turn = m * SLOT_USES[self.slot] + q
                self.n = m * NCH + self.i

        class Pair:

            def __init__(self, m, quad, u):
                quad, self.half = quad + u // 2, u % 2
                self.chunks = [Chunk(m, quad, 2 * self.half + k) for k in range(2)]
                self.turn = m * HALF_USES[self.half] + quad
                self.other_turn = m * HALF_USES[1 - self.half] + quad + self.half
                self.n = m * NPAIR + 2 * quad + self.half
                self.m, self.quad = m, quad
                self.tiles = ds((quad * SL + 2 * self.half) * TC, 2 * TC)

        def paired(m_, eng, step):
            L = (NPAIR - 2) // 2
            at = lambda i, quad=0: Pair(m_, quad + i // 2, i % 2)
            step(at(0), None, at(1))
            with eng.Fori(0, L) as quad:
                for i in range(1, 3):
                    step(at(i, quad), at(i - 1, quad), at(i + 1, quad))
            for i in range(2 * L + 1, NPAIR):
                step(at(i), at(i - 1), at(i + 1) if i + 1 < NPAIR else None)
            step(None, at(NPAIR - 1), None)

        class Group:

            def __init__(self, it, b, phase=0):
                self.it, self.b = it, b
                self.i = it * 2 + b
                self.n = self.i + phase * NG
                self.turn = it + phase * (NG // 2)

        def lagged(eng, step, phase=0):
            L = (NG - 4) // 2
            at = lambda i, it=0: Group(it + i // 2, i % 2, phase)
            for i in range(3):
                step(at(i), at(i - 1) if i else None, at(i + 1))
            with eng.Fori(0, L) as it:
                for i in range(3, 5):
                    step(at(i, it), at(i - 1, it), at(i + 1, it))
            for i in range(2 * L + 3, NG):
                step(at(i), at(i - 1), at(i + 1) if i + 1 < NG else None)
            step(None, at(NG - 1), None)

        def all_groups(eng, step, phase=0):
            for b in range(2):
                step(Group(0, b, phase))
            with eng.Fori(1, NG // 2) as it:
                for b in range(2):
                    step(Group(it, b, phase))

        def wait_if(eng, semaphore, count):
            if not (isinstance(count, int) and count == 0):
                eng.wait_ge(semaphore, count)

        def all_chunks(eng, m, step):
            with eng.Fori(0, NCH // SL) as quad:
                for u in range(SL):
                    step(Chunk(m, quad, u))
            for u in range(NCH % SL):
                step(Chunk(m, NCH // SL, u))

        def pipelined(m_, eng, step):
            L = (NCH - 3) // SL
            at = lambda i, quad=0: Chunk(m_, quad + i // SL, i % SL)
            step(at(0), None, None, at(1))
            step(at(1), at(0), None, at(2))
            with eng.Fori(0, L) as quad:
                for i in range(2, SL + 2):
                    step(*(at(k, quad) for k in (i, i - 1, i - 2, i + 1)))
            for i in range(2 + SL * L, NCH):
                step(at(i), at(i - 1), at(i - 2), at(i + 1) if i + 1 < NCH else None)
            step(None, at(NCH - 1), at(NCH - 2), None)
            step(None, None, at(NCH - 1), None)

        def all_free(eng, *semaphores):
            for semaphore in semaphores:
                eng.nop(nofuse=True).then_inc(semaphore, 1)

        def hold(eng):
            eng.nop(nofuse=True)

        def number_of_passes(eng):
            eng.wait_ge(passes_set, 1)
            return eng.value_load(passes_i[0:1, 0:1], min_val=1, max_val=MAXPASS)

        def window_start(eng, c):
            return eng.value_load(base_i[0:1, ds(c.i, 1)], min_val=0, max_val=TOP)

        def node_rows(t, group):
            return t[ds(group * (TPG * P), TPG * P), :].rearrange("(j p) d -> p j d", p=P)

        def wide(ap, n):
            p, a = ap.shape
            return ap.rearrange("p (a b) -> p a b", b=1).broadcast_to([p, a, n])

        def tiled(ap, n):
            p, a = ap.shape
            return ap.rearrange("p (b a) -> p b a", b=1).broadcast_to([p, n, a])

        @block.sync
        def _(sp):
            def load_x(k):
                sp.dma_start(x_in[:, k.b, :, :], node_rows(x, k.i)).then_inc(x_in_moved[k.b], 16)

            load_x(Group(0, 0))
            load_x(Group(0, 1))
            for there, source in w_node_parts:
                sp.dma_start(there, source).then_inc(node_consts_landed, 16)
            sp.wait_ge(zeroed, 1)
            for there, source in bias_node_parts:
                sp.dma_start(there, source).then_inc(node_consts_landed, 16)
            sp.dma_start(dst_rows[:, :, :], dst_c.rearrange("(q k) e -> q k e", q=QP)).then_inc(dst_landed, 16)

            def store_tables(k):
                b = k.b
                sp.wait_ge(pqr_biased, 2 * k.n + 2)
                hold(sp)
                sp.dma_start(node_rows(p_tab, k.i), pqr[b][:, :, 0:H1]).then_inc(p_stored[b], 16)
                sp.wait_ge(lo_done, k.n + 1)
                hold(sp)
                for t, part in enumerate((qr_hi, qr_mid, qr_lo)):
                    sp.dma_start(node_rows(qr_tab[t], k.i), part[b][:, :, :]).then_inc(parts_stored[b], 16)

            def step(k, before):
                sp.wait_ge(res_done[k.b], k.turn + 1)
                hold(sp)
                load_x(Group(k.it + 1, k.b))
                if before:
                    store_tables(before)

            last = NG // 2 - 1
            step(Group(0, 0), None)
            sp.dma_start(dst_f[:, :].bitcast(i32), dst_t).then_inc(dstf_landed, 16)
            step(Group(0, 1), Group(0, 0))
            sp.wait_ge(zeroed, 4)
            for there, source in edge_consts[:N_CONST // 2]:
                sp.dma_start(there, source).then_inc(consts_landed, 16)
            step(Group(1, 0), Group(0, 1))
            for there, source in edge_consts[N_CONST // 2:]:
                sp.dma_start(there, source).then_inc(consts_landed, 16)

            sp.wait_ge(range_set, 3)
            sp.dma_start(base_d, least[:, :]).then_inc(range_stored, 16)
            sp.dma_start(range_d, most[:, :]).then_inc(range_stored, 16)
            sp.wait_ge(range_stored, 32)
            sp.dma_start(range_row[0:1, :], range_d.rearrange("q k -> (q k)").partition_broadcast(1)).then_inc(range_back, 16)
            sp.dma_start(base0[:, :], base_d.rearrange("q k -> (q k)").partition_broadcast(P)).then_inc(range_back, 16)

            pieces = last - 2
            cols = NCH * TC // pieces
            assert NCH * TC % pieces == 0
            with sp.Fori(1, last - 1) as it:
                piece = ds(it * cols - cols, cols)
                step(Group(it, 1), Group(it, 0))
                sp.dma_start(et_key[:, piece].bitcast(i32), etype_t[:, piece]).then_inc(ids_landed, 16)
                step(Group(it + 1, 0), Group(it, 1))
                sp.dma_start(w_f[:, piece], weight_t[:, piece]).then_inc(weight_landed, 16)
            step(Group(last - 1, 1), Group(last - 1, 0))
            for k in (Group(last - 1, 1), Group(last, 0), Group(last, 1)):
                store_tables(k)
            sp.wait_ge(parts_stored[0], 48 * (NG // 2))

            passes = number_of_passes(sp)

            def layer0_pass(m):
                sp.wait_ge(pass_ready, m + 1)
                hold(sp)

                def step(c):
                    s = c.slot
                    sp.wait_ge(h1_summed[s], c.turn + 1)
                    hold(sp)
                    sp.dma_start(idx[s][:, :], src_t[:, ds(c.i * TC, TC)]).then_inc(idx_landed[s], 16)
                    sp.dma_start(ea[s][:, :], edge_cols[ds(c.i, 1), :, :].rearrange("c p n -> (c p) n")).then_inc(ea_landed[s], 16)
                    sp.wait_ge(hot_built[s], c.turn + 1)
                    hold(sp)
                    sp.dma_start(dst_wide[s], dst_c[ds(c.i, 1), :].rearrange("c e -> (c e)").partition_broadcast(3 * W))\
                      .then_inc(dst_wide_landed[s], 16)
                    sp.wait_ge(parts_stored[1], 48 * (NG // 2))
                    start = window_start(sp, c)
                    sp.wait_ge(h2_summed[s], c.turn + 1)
                    hold(sp)
                    sp.dma_start(qr_w[s][:, :], qr_tab[:, ds(start, W), :]).then_inc(qr_landed[s], 16)

                all_chunks(sp, m, step)

            with sp.Fori(0, passes) as m:
                layer0_pass(m)

            with sp.Fori(0, NG // 2) as it:
                for b in range(2):
                    sp.wait_ge(mid_h_done[b], it + 1)
                    hold(sp)
                    sp.dma_start(node_rows(h_tab, it * 2 + b), x_in[:, b, :, :]).then_inc(x_in_moved[b], 16)
            for b in range(2):
                sp.wait_ge(x_in_moved[b], 2 * MOVES)

            passes = number_of_passes(sp)

            def layer1_pass(m):
                def step(c):
                    s = c.slot
                    sp.wait_ge(scattered[s], c.turn + 1)
                    hold(sp)
                    sp.dma_start(idx[s][:, :], src_t[:, ds(c.i * TC, TC)]).then_inc(idx1_landed[s], 16)

                all_chunks(sp, m, step)

            with sp.Fori(0, passes) as m:
                layer1_pass(m)

            with sp.Fori(0, NG // 2) as it:
                for b in range(2):
                    g = it * 2 + b
                    if b == 0:
                        sp.wait_ge(fin_even, 2 * it + 2)
                    else:
                        sp.wait_ge(fin_odd, it + 2)
                    hold(sp)
                    sp.dma_start(node_rows(out, g), res[:, ds(g * TPG, TPG), :]).then_inc(out_stored, 16)
            sp.wait_ge(out_stored, 16 * NG)

        @block.gpsimd
        def _(pool):
            all_free(pool, fin_odd)
            pool.memset(bias_node[:, 0:H1], 0.0).then_inc(zeroed, 1)
            pool.memset(w1_pair[:, :, :], 0.0).then_inc(zeroed, 1)
            pool.memset(w2_tile[:, :, :], 0.0).then_inc(zeroed, 1)
            pool.memset(wn2_half[:, :, :], 0.0).then_inc(zeroed, 1)
            pool.iota(iota_i[:, :], [[1, W]], base=0, channel_multiplier=0).then_inc(ramps_set, 1)
            pool.iota(iota_key_i[:, :, :], [[KEY, R], [1, W]], base=1, channel_multiplier=0).then_inc(ramps_set, 1)
            for k in range(3):
                pool.wait_ge(ramps_set, k + 2)
                pool.iota(row_i[k * W:(k + 1) * W, :], [[0, 1]], base=0, channel_multiplier=1).then_inc(ramps_set, 1)
            pool.wait_ge(ramps_set, 5)
            pool.memset(ident[:, :], 0.0).then_inc(ident_set, 1)
            pool.wait_ge(ident_set, 1)
            pool.affine_select(out=ident[:, :], in_=ident[:, :], compare_op=ALU.not_equal, fill=1.0, base=0,
                               pattern=[[-1, P]], channel_multiplier=1).then_inc(ident_set, 1)
            pool.iota(pass_i[:, :], [[W, MAXPASS]], base=0, channel_multiplier=0).then_inc(ramps_set, 1)

            def gather(c, table, rows_of, used, idx_there, landed):
                s = c.slot
                pool.wait_ge(used[s], c.turn + 1)
                hold(pool)
                pool.wait_ge(idx_there[s], 16 * c.turn + 16)
                hold(pool)
                for t in range(TC):
                    pool.indirect_dma_start(
                        out=rows_of[s][:, t, :], out_offset=None, in_=table,
                        in_offset=bass.IndirectOffsetOnAxis(ap=idx[s][:, t:t + 1], axis=0),
                    ).then_inc(landed[s], 16)

            def step(group, before, after):
                if group:
                    b = group.b
                    pool.wait_ge(x_in_moved[b], 16 * group.turn + 16)
                    pool.wait_ge(h_done, group.n + 1)
                    pool.tensor_tensor(res[:, ds(group.i * TPG, TPG), :], h[b], x_in[:, b, :, :], ALU.add).then_inc(res_done[b], 1)
                if before:
                    b = before.b
                    pool.wait_ge(hi_done, before.n + 1)
                    pool.tensor_tensor(qr_res[b], pqr[b][:, :, H1:P], qr_hi[b], ALU.subtract).then_inc(res1_done, 1)
                    pool.wait_ge(mid_done, before.n + 1)
                    pool.tensor_tensor(qr_lo[b], qr_res[b], qr_mid[b], ALU.subtract).then_inc(lo_done, 1)

            lagged(pool, step)

            for b in range(2):
                pool.wait_ge(p_stored[b], 16 * (NG // 2))
            pool.wait_ge(parts_stored[0], 48 * (NG // 2))
            passes = number_of_passes(pool)
            with pool.Fori(0, passes) as m:
                all_chunks(pool, m, lambda c: gather(c, p_tab, prow, h1_summed, idx_landed, prow_landed))

            def centre(k):
                pool.wait_ge(aggr_done, k.n + 1)
                hold(pool)
                pool.wait_ge(x_in_moved[k.b], MOVES + 16 * k.it)
                pool.tensor_tensor(x_in[:, k.b, :, :], res[:, ds(k.i * TPG, TPG), :], wide(mv[:, k.b, :, 0], D), ALU.subtract)\
                    .then_inc(mid_centred[k.b], 1)

            all_groups(pool, centre, phase=1)

            for b in range(2):
                pool.wait_ge(x_in_moved[b], 2 * MOVES)
            passes = number_of_passes(pool)
            with pool.Fori(0, passes) as m:
                all_chunks(pool, m, lambda c: gather(c, h_tab, rows, scattered, idx1_landed, rows_landed))

            with pool.Fori(0, NG // 2) as it:
                pool.wait_ge(fin_relu, 2 * it + 2)
                there = res[:, ds((it * 2 + 1) * TPG, TPG), :]
                pool.tensor_tensor(there, there, x_in[:, 1, :, :], ALU.add).then_inc(fin_odd, 1)

        @block.scalar
        def _(act):
            all_free(act, *sums_copied)

            def std_of(k):
                act.wait_ge(eps_added, k.n + 1)
                act.activation(std[:, k.b, :], var_eps[:, k.b, :], ACT.Sqrt).then_inc(std_done, 1)

            def step(group, before, after):
                if group:
                    b = group.b
                    act.wait_ge(h_transposed[b], 2 * group.turn + 1)
                    act.activation(hT[:, 0:4 * P], bank[0][:, 0:4 * P], ACT.Copy).then_inc(hT_copied, 1)
                    act.wait_ge(h_transposed[b], 2 * group.turn + 2)
                    act.activation(hT[:, 4 * P:TPG * P], bank[1][:, 0:(TPG - 4) * P], ACT.Copy).then_inc(hT_copied, 1)
                if before:
                    b = before.b
                    act.wait_ge(pqr_biased, 2 * before.n + 2)
                    act.activation(qr_hi[b], pqr[b][:, :, H1:P], ACT.Copy).then_inc(hi_done, 1)
                if after:
                    std_of(after)
                if before:
                    act.wait_ge(res1_done, before.n + 1)
                    act.activation(qr_mid[b], qr_res[b], ACT.Copy).then_inc(mid_done, 1)

            std_of(Group(0, 0))
            lagged(act, step)
            act.wait_ge(dstf_landed, 16)
            act.activation(dst_f[:, :], dst_f[:, :].bitcast(i32), ACT.Copy).then_inc(edges_set, 1)

            def relu_h2(c):
                act.wait_ge(h2_summed[c.slot], c.turn + 2)
                act.activation(h2_sb[:, :], ps_h2[:, 0:2 * P], ACT.Relu).then_inc(h2_done, 1)

            def copy_tile_sums(c):
                act.wait_ge(tiles_summed, c.n + 1)
                act.activation(tile_sums[:, :], ps_tiles[:, 0:D], ACT.Copy).then_inc(tiles_copied, 1)

            def relu_msg1(c):
                act.wait_ge(msg1_summed, c.n + 1)
                act.activation(msg1_sb[:, :], ps_msg1[:, :], ACT.Relu, bias=be2_col[:, 0:1]).then_inc(msg1_done, 1)

            def relu_msg2(c):
                act.wait_ge(msg2_biased, c.n + 1)
                act.activation(msg2_sb[:, :], msg2_sb[:, :], ACT.Relu).then_inc(msg2_done, 1)

            act.wait_ge(consts_landed, 16 * N_CONST)
            passes = number_of_passes(act)

            def step(c, before, before2, after):
                if before:
                    relu_h2(before)
                if before2:
                    copy_tile_sums(before2)
                if c:
                    relu_msg1(c)
                if before:
                    relu_msg2(before)

            with act.Fori(0, passes) as m:
                pipelined(m, act, step)

            def stage_agg(it, g, b):
                wait_if(act, agg_transposed[b], 2 * it)
                act.activation(agg_group[b][:, :], agg[:, ds(g * (TPG * P), TPG * P)], ACT.Copy).then_inc(agg_staged[b], 1)

            act.wait_ge(agg_added, passes * NCH + 1)
            stage_agg(0, 0, 0)

            def step(group, before, after):
                if after:
                    stage_agg(after.it, after.i, after.b)
                if group:
                    std_of(group)
                if before:
                    b = before.b
                    act.wait_ge(rstd_done, before.n + 1)
                    act.wait_ge(mid_centred[b], before.it + 1)
                    for j in range(TPG):
                        ins = act.activation(x_in[:, b, j, :], x_in[:, b, j, :], ACT.Relu, scale=rstd[:, b, j:j + 1])
                    ins.then_inc(mid_h_done[b], 1)

            lagged(act, step, phase=1)
            act.wait_ge(ids_landed, 16 * (NG // 2 - 3))
            act.activation(et_key[:, :], et_key[:, :].bitcast(i32), ACT.Copy, scale=float(KEY), bias=1.0).then_inc(edges_set, 1)

            def copy_sums(p):
                for k, c in enumerate(p.chunks):
                    if k == 0:
                        act.wait_ge(projected[p.half], p.turn + 1)
                    act.wait_ge(scattered[c.slot], c.turn + 2)
                    act.activation(rel_sums[p.half][:, :, k, :],
                                   bank[c.slot][:, 0:RW].rearrange("p (r n) -> p r n", n=W), ACT.Copy)
                    act.activation(w_sums[p.half][:, k, :], bank[c.slot][0:R, RW:RW + W], ACT.Copy)\
                       .then_inc(sums_copied[c.slot], 1)

            with act.Fori(0, passes) as m:
                with act.Fori(0, NPAIR // 2) as quad:
                    for u in range(2):
                        copy_sums(Pair(m, quad, u))
                for u in range(NPAIR % 2):
                    copy_sums(Pair(m, NPAIR // 2, u))

            for b in range(2):
                act.wait_ge(pair_added[b], passes * HALF_USES[b] + 1)
            def relu_odd(it):
                act.wait_ge(fin_odd, it + 1)
                for a, (t0, t1) in enumerate(HALVES):
                    act.wait_ge(agg_transposed[1], 2 * (it + NG // 2) + a + 1)
                    act.activation(x_in[:, 1, t0:t1, :], bank[2 + a][:, 0:(t1 - t0) * P].rearrange("p (j d) -> p j d", d=D),
                                   ACT.Relu).then_inc(fin_relu, 1)

            stage_agg(NG // 2, 0, 0)
            with act.Fori(0, NG // 2 - 1) as it:
                stage_agg(it + NG // 2, it * 2 + 1, 1)
                stage_agg(it + 1 + NG // 2, it * 2 + 2, 0)
                relu_odd(it)
            stage_agg(NG - 1, NG - 1, 1)
            relu_odd(NG // 2 - 1)

        @block.vector
        def _(dve):
            all_free(dve, *hot_built, *pair_added)

            def statistics(k, there):
                b = k.b
                for j in range(TPG):
                    ins = dve.bn_stats(stats[:, b, j, :], there(j))
                ins.then_inc(stats_done, 1)
                dve.wait_ge(stats_done, k.n + 1)
                hold(dve)
                for j in range(TPG):
                    ins = dve.bn_aggr(mv[:, b, j, :], stats[:, b, j, :])
                ins.then_inc(aggr_done, 1)
                dve.wait_ge(aggr_done, k.n + 1)
                dve.tensor_scalar_add(var_eps[:, b, :], mv[:, b, :, 1], EPS).then_inc(eps_added, 1)

            def reciprocals(k):
                dve.wait_ge(std_done, k.n + 1)
                dve.reciprocal(rstd[:, k.b, :], std[:, k.b, :]).then_inc(rstd_done, 1)

            def first_norm(k):
                b = k.b
                dve.wait_ge(x_in_moved[b], 16 * k.turn + 16)
                hold(dve)
                statistics(k, lambda j: x_in[:, b, j, :])
                wait_if(dve, h_transposed[b], 2 * k.turn)
                wait_if(dve, res_done[b], k.turn)
                dve.tensor_tensor(h[b], x_in[:, b, :, :], wide(mv[:, b, :, 0], D), ALU.subtract).then_inc(centred, 1)
                reciprocals(k)
                dve.wait_ge(rstd_done, k.n + 1)
                dve.wait_ge(centred, k.n + 1)
                dve.scalar_tensor_tensor(out=h[b], in0=h[b], scalar=0.0, in1=wide(rstd[:, b, :], D),
                                         op0=ALU.max, op1=ALU.mult).then_inc(h_done, 1)

            def add_bias(k):
                b = k.b
                wait_if(dve, p_stored[b], 16 * k.turn)
                wait_if(dve, parts_stored[b], 48 * k.turn)
                for a, (t0, t1) in enumerate(HALVES):
                    dve.wait_ge(pqr_ready, 2 * k.n + a + 1)
                    dve.tensor_tensor(pqr[b][:, t0:t1, :], bank[2 + a][:, 0:(t1 - t0) * P].rearrange("p (j d) -> p j d", d=P),
                                      tiled(bias_node[:, :], t1 - t0), ALU.add).then_inc(pqr_biased, 1)

            def least_and_range():
                dve.wait_ge(dst_landed, 16)
                dve.tensor_reduce(least[:, :], dst_rows[:, :, :].bitcast(u32), AX.X, ALU.min).then_inc(range_set, 1)
                dve.tensor_reduce(most[:, :], dst_rows[:, :, :], AX.X, ALU.max).then_inc(range_set, 1)
                dve.wait_ge(range_set, 2)
                dve.tensor_tensor(most[:, :], most[:, :], least[:, :], ALU.subtract).then_inc(range_set, 1)

            def ramps():
                dve.wait_ge(ramps_set, 6)
                dve.tensor_copy(iota_key[:, :, :], iota_key_i[:, :, :])
                dve.tensor_copy(iota_f[:, :], iota_i[:, :]).then_inc(prep_step, 1)
                dve.tensor_copy(row_f[:, :], row_i[:, :])
                dve.tensor_copy(pass_f[:, :], pass_i[:, :]).then_inc(prep_step, 1)
                dve.wait_ge(ident_set, 2)
                dve.tensor_tensor(fold_tiles[:, :], ident[:, 0:W], ident[:, W:2 * W], ALU.add).then_inc(fold_step, 1)
                for t in range(2, TC):
                    dve.wait_ge(fold_step, t - 1)
                    dve.tensor_tensor(fold_tiles[:, :], fold_tiles[:, :], ident[:, t * W:(t + 1) * W], ALU.add).then_inc(fold_step, 1)

            def step(group, before, after):
                if group:
                    first_norm(group)
                if before:
                    add_bias(before)
                if group and isinstance(group.i, int) and group.i == 0:
                    ramps()
                    dve.wait_ge(node_consts_landed, 16 * N_NODE_CONST)
                if group and isinstance(group.i, int) and group.i == 1:
                    least_and_range()

            lagged(dve, step)

            dve.wait_ge(range_back, 32)
            dve.tensor_reduce(range_max[:, :], range_row[:, :], AX.X, ALU.max).then_inc(prep_step, 1)
            dve.tensor_scalar_add(base0[:, :], base0[:, :], -float(W)).then_inc(prep_step, 1)
            dve.wait_ge(prep_step, 4)
            dve.tensor_scalar(pass_f[:, :], pass_f[:, :], range_max[0:1, 0:1], None, ALU.is_le).then_inc(prep_step, 1)
            dve.wait_ge(prep_step, 5)
            dve.tensor_reduce(passes_f[:, :], pass_f[:, :], AX.X, ALU.add).then_inc(prep_step, 1)
            dve.wait_ge(prep_step, 6)
            dve.tensor_copy(passes_i[:, :], passes_f[:, :]).then_inc(passes_set, 1)

            def set_windows(m, step, ready):
                dve.tensor_scalar_add(base_f[:, :], base_f[:, :], float(W)).then_inc(step, 1)
                dve.wait_ge(step, 2 * m + 1)
                dve.tensor_scalar_min(base_c[:, :], base_f[:, :], float(TOP)).then_inc(step, 1)
                dve.wait_ge(step, 2 * m + 2)
                dve.tensor_copy(base_i[:, :], base_c[:, :]).then_inc(ready, 1)

            def match_window(c):
                return dve.scalar_tensor_tensor(
                    out=hot[c.slot][:, :, :], in0=tiled(iota_f[:, 0:W], TC), scalar=base_c[:, ds(c.i, 1)],
                    in1=wide(dst_f[:, ds(c.i * TC, TC)], W), op0=ALU.add, op1=ALU.is_equal)

            dve.wait_ge(prep_step, 4)
            dve.tensor_copy(base_f[:, :], base0[:, :]).then_inc(prep_step, 1)
            dve.wait_ge(prep_step, 7)
            set_windows(0, pass_step, pass_ready)
            dve.memset(agg[:, tables_from + TABLES:NPAD], 0.0)
            dve.memset(agg[:, 0:tables_from], 0.0)
            dve.wait_ge(parts_stored[1], 48 * (NG // 2))
            dve.memset(agg[:, tables_from:tables_from + TABLES], 0.0).then_inc(agg_added, 1)
            dve.wait_ge(consts_landed, 16 * N_CONST)
            dve.wait_ge(edges_set, 1)
            passes = number_of_passes(dve)

            def build_hot(c):
                s = c.slot
                match_window(c)
                dve.wait_ge(dst_wide_landed[s], 16 * c.turn + 16)
                hold(dve)
                dve.tensor_scalar(hotT[s % 2][:, :], dst_wide[s], base_c[0:3 * W, ds(c.i, 1)], row_f[:, 0:1],
                                  ALU.subtract, ALU.is_equal).then_inc(hot_built[s], 1)

            def relu_h1(c):
                dve.wait_ge(h1_summed[c.slot], c.turn + 2)
                dve.tensor_scalar_max(h1_sb[:, :], ps_h1[:, 0:P], 0.0).then_inc(h1_done, 1)

            def add_chunk(c):
                start = window_start(dve, c)
                dve.wait_ge(chunk_summed, c.n + 1)
                dve.wait_ge(agg_added, c.n + 1)
                dve.tensor_tensor(agg[:, ds(start, W)], agg[:, ds(start, W)], ps_agg[:, 0:W], ALU.add).then_inc(agg_added, 1)

            def bias_msg2(c):
                dve.wait_ge(msg2_summed, c.n + 1)
                dve.tensor_tensor(msg2_sb[:, :], ps_msg2[:, :], bn2_rep[:, :], ALU.add).then_inc(msg2_biased, 1)

            def step(c, before, before2, after):
                if c:
                    relu_h1(c)
                if after:
                    build_hot(after)
                if before2:
                    add_chunk(before2)
                if before:
                    bias_msg2(before)

            with dve.Fori(0, passes) as m:
                dve.wait_ge(pass_ready, m + 1)
                hold(dve)
                build_hot(Chunk(m, 0, 0))
                pipelined(m, dve, step)
                set_windows(m + 1, pass_step, pass_ready)

            def step(group, before, after):
                if group:
                    b = group.b
                    for a, (t0, t1) in enumerate(HALVES):
                        there = res[:, ds(group.i * TPG + t0, t1 - t0), :]
                        dve.wait_ge(agg_transposed[b], 2 * group.it + a + 1)
                        dve.tensor_tensor(there, there, bank[2 * b + a][:, 0:(t1 - t0) * P].rearrange("p (j d) -> p j d", d=D),
                                          ALU.add).then_inc(mid_added[b], 1)
                    dve.wait_ge(mid_added[b], 2 * group.it + 2)
                    hold(dve)
                    wait_if(dve, mid_centred[b], group.it)
                    hold(dve)
                    statistics(group, lambda j: res[:, ds(group.i * TPG + j, 1), :].rearrange("p j d -> p (j d)"))
                if before:
                    wait_if(dve, mid_h_done[before.b], before.it)
                    hold(dve)
                    reciprocals(before)

            lagged(dve, step, phase=1)

            for b in range(2):
                dve.wait_ge(agg_staged[b], NG // 2)
            dve.memset(agg[:, :], 0.0).then_inc(agg_cleared, 1)
            dve.wait_ge(agg_cleared, 1)
            dve.wait_ge(weight_landed, 16 * (NG // 2 - 3))
            dve.wait_ge(edges_set, 2)
            dve.tensor_copy(base_f[:, :], base0[:, :]).then_inc(prep_step, 1)
            dve.wait_ge(prep_step, 8)

            def build_hot1(p):
                k = p.half
                for n, c in enumerate(p.chunks):
                    dve.tensor_scalar(offset[k][:, n * TC:(n + 1) * TC], dst_f[:, ds(c.i * TC, TC)], base_c[:, ds(c.i, 1)],
                                      -1.0, ALU.subtract, ALU.max).then_inc(offsets_set, 1)
                for n, c in enumerate(p.chunks):
                    dve.wait_ge(scattered[c.slot], c.turn + 1)
                    match_window(c)
                    for t in range(TC):
                        at = ds(c.i * TC + t, 1)
                        dve.tensor_scalar(et_w[c.slot][:, t, :], iota_key[:, :, 0], et_key[:, at], w_f[:, at],
                                          ALU.is_equal, ALU.mult)
                dve.wait_ge(offsets_set, 2 * p.n + 2)
                dve.scalar_tensor_tensor(out=key[k][:, :], in0=offset[k][:, :], scalar=float(W), in1=et_key[:, p.tiles],
                                         op0=ALU.min, op1=ALU.add).then_inc(keys_set, 1)
                dve.wait_ge(keys_set, p.n + 1)
                for n, c in enumerate(p.chunks):
                    u = c.slot
                    if p.half:
                        dve.wait_ge(scattered[u - 2], p.m * SLOT_USES[u - 2] + p.quad + 2)
                    else:
                        dve.wait_ge(scattered[u + 2], p.m * SLOT_USES[u + 2] + p.quad + 1)
                        dve.wait_ge(scattered[u], c.turn + 1)
                    for t in range(TC):
                        ins = dve.tensor_scalar(hot_rel[u % 2][:, t, :], iota_key[:, :, :].rearrange("p r n -> p (r n)"),
                                                key[k][:, n * TC + t:n * TC + t + 1], w_f[:, ds(c.i * TC + t, 1)],
                                                ALU.is_equal, ALU.mult)
                    ins.then_inc(hot1_built[u], 1)

            def add_pair(p):
                for n, c in enumerate(p.chunks):
                    start = window_start(dve, c)
                    dve.wait_ge(projected[p.half], p.turn + 2)
                    if n == 0:
                        dve.wait_ge(pair_added[p.half], p.turn + 1)
                        dve.wait_ge(pair_added[1 - p.half], p.other_turn + 1)
                    else:
                        dve.wait_ge(half_added, p.n + 1)
                    dve.tensor_tensor(agg[:, ds(start, W)], agg[:, ds(start, W)], bank[4 + p.half][:, n * W:(n + 1) * W],
                                      ALU.add).then_inc(pair_added[p.half] if n else half_added, 1)

            def step1(pair, before, after):
                if after:
                    build_hot1(after)
                if before:
                    add_pair(before)

            with dve.Fori(0, passes) as m:
                set_windows(m, pass1_step, pass1_ready)
                dve.wait_ge(pass1_ready, m + 1)
                hold(dve)
                build_hot1(Pair(m, 0, 0))
                paired(m, dve, step1)

            with dve.Fori(0, NG // 2) as it:
                for a, (t0, t1) in enumerate(HALVES):
                    dve.wait_ge(agg_transposed[0], 2 * (it + NG // 2) + a + 1)
                    there = res[:, ds(it * 2 * TPG + t0, t1 - t0), :]
                    dve.scalar_tensor_tensor(
                        out=there, in0=bank[a][:, 0:(t1 - t0) * P].rearrange("p (j d) -> p j d", d=D),
                        scalar=0.0, in1=there, op0=ALU.max, op1=ALU.add)\
                       .then_inc(fin_even, 1)

        @block.tensor
        def _(pe):
            all_free(pe, *h1_summed, *h2_summed, *scattered, *projected)
            pe.wait_ge(ident_set, 2)

            def transpose_agg(k, before, added):
                b = k.b
                pe.wait_ge(agg_staged[b], before + 1)
                wait_if(pe, added[b], 2 * k.it)
                for a, (t0, t1) in enumerate(HALVES):
                    for j in range(t0, t1):
                        ins = pe.transpose(bank[2 * b + a][:, (j - t0) * P:(j - t0 + 1) * P],
                                           agg_group[b][:, j * P:(j + 1) * P], ident[:, :])
                    ins.then_inc(agg_transposed[b], 1)

            pe.wait_ge(node_consts_landed, 16 * N_NODE_CONST)

            def step(k):
                pe.wait_ge(h_done, k.n + 1)
                wait_if(pe, hT_copied, 2 * k.n)
                for a, (t0, t1) in enumerate(HALVES):
                    for j in range(t0, t1):
                        ins = pe.transpose(bank[a][:, (j - t0) * P:(j - t0 + 1) * P], h[k.b][:, j, :], ident[:, :])
                    ins.then_inc(h_transposed[k.b], 1)
                wait_if(pe, pqr_biased, 2 * k.n)
                for a, (t0, t1) in enumerate(HALVES):
                    pe.wait_ge(hT_copied, 2 * k.n + a + 1)
                    for j in range(t0, t1):
                        ins = pe.matmul(bank[2 + a][:, (j - t0) * P:(j - t0 + 1) * P],
                                        hT[:, j * P:(j + 1) * P], w_node[:, :], start=True, stop=True)
                    ins.then_inc(pqr_ready, 1)

            all_groups(pe, step)
            pe.wait_ge(consts_landed, 16 * N_CONST)
            pe.wait_ge(fold_step, TC - 1)

            def sum_h1(c):
                s = c.slot
                pe.wait_ge(ea_landed[s], 16 * c.turn + 16)
                for q in range(2):
                    pe.matmul(ps_h1[:, 0:P], w1_pair[:, q, :], ea[s][:, q * P:(q + 1) * P], start=(q == 0), stop=False)
                pe.wait_ge(qr_landed[s], 16 * c.turn + 16)
                pe.wait_ge(hot_built[s], c.turn + 2)
                for t in range(TC):
                    pe.matmul(ps_h1[t * H1:(t + 1) * H1, 0:P], qr_w[s][:, 0:H1], hotT[s % 2][:, t * P:(t + 1) * P],
                              start=False, stop=False)
                pe.wait_ge(prow_landed[s], 16 * TC * c.turn + 16 * TC)
                pe.matmul(ps_h1[:, 0:P], prow[s][:, :, :].rearrange("p t o -> p (t o)"), ident[:, :], start=False, stop=True)\
                  .then_inc(h1_summed[s], 1)

            def sum_msg1(c):
                pe.wait_ge(h1_done, c.n + 1)
                for t in range(TC):
                    ins = pe.matmul(ps_msg1[:, t * P:(t + 1) * P], w2_tile[:, t, :], h1_sb[:, :], start=True, stop=True)
                ins.then_inc(msg1_summed, 1)

            def sum_h2(c):
                s = c.slot
                pe.wait_ge(msg1_done, c.n + 1)
                for a in range(2):
                    there = ps_h2[a * H2:(a + 1) * H2, 0:2 * P]
                    cols = slice(a * 2 * P, (a + 1) * 2 * P)
                    pe.matmul(there, wn1_msg[:, :], msg1_sb[:, cols], start=True, stop=False)
                    ins = pe.matmul(there, qr_w[s][:, H1:QR], hotT[s % 2][:, cols], start=False, stop=True)
                ins.then_inc(h2_summed[s], 1)

            def sum_msg2(c):
                pe.wait_ge(h2_done, c.n + 1)
                for t in range(TC):
                    a, b = t // 2, t % 2
                    ins = pe.matmul(ps_msg2[:, t * P:(t + 1) * P], h2_sb[:, b * P:(b + 1) * P], wn2_half[:, a, :],
                                    start=True, stop=True)
                ins.then_inc(msg2_summed, 1)

            def sum_tiles(c):
                pe.wait_ge(msg2_done, c.n + 1)
                for t in range(TC):
                    ins = pe.matmul(ps_tiles[t * W:(t + 1) * W, 0:D], hot[c.slot][:, t, :], msg2_sb[:, t * P:(t + 1) * P],
                                    start=True, stop=True)
                ins.then_inc(tiles_summed, 1)

            def sum_chunk(c):
                pe.wait_ge(tiles_copied, c.n + 1)
                pe.wait_ge(agg_added, c.n + 1)
                pe.matmul(ps_agg[:, 0:W], tile_sums[:, :], fold_tiles[:, :], start=True, stop=True).then_inc(chunk_summed, 1)

            passes = number_of_passes(pe)

            def step(c, before, before2, after):
                if before:
                    sum_h2(before)
                if c:
                    sum_h1(c)
                if before2:
                    sum_tiles(before2)
                if c:
                    sum_msg1(c)
                if before2:
                    sum_chunk(before2)
                if before:
                    sum_msg2(before)

            with pe.Fori(0, passes) as m:
                pipelined(m, pe, step)

            all_groups(pe, lambda k: transpose_agg(k, k.it, mid_added))

            def scatter(c):
                s = c.slot
                pe.wait_ge(hot1_built[s], c.turn + 1)
                pe.wait_ge(rows_landed[s], 16 * TC * c.turn + 16 * TC)
                pe.wait_ge(sums_copied[s], c.turn + 1)
                for t in range(TC):
                    pe.matmul(bank[s][:, 0:RW], rows[s][:, t, :], hot_rel[s % 2][:, t, :], start=(t == 0), stop=(t == TC - 1))
                for t in range(TC):
                    ins = pe.matmul(bank[s][0:R, RW:RW + W], et_w[s][:, t, :], hot[s][:, t, :],
                                    start=(t == 0), stop=(t == TC - 1))
                ins.then_inc(scattered[s], 1)

            def project(p):
                for c in p.chunks:
                    pe.wait_ge(sums_copied[c.slot], c.turn + 2)
                pe.wait_ge(pair_added[p.half], p.turn + 1)
                there = bank[4 + p.half][:, 0:2 * W]
                for r in range(R):
                    pe.matmul(there, w_rel_sb[:, r, :], rel_sums[p.half][:, r, :, :].rearrange("p c n -> p (c n)"),
                              start=(r == 0), stop=False)
                pe.matmul(there, b_rel_sb[:, :], w_sums[p.half][:, :, :].rearrange("p c n -> p (c n)"), start=False, stop=True)\
                  .then_inc(projected[p.half], 1)

            def step1(pair, before, after):
                if pair:
                    for c in pair.chunks:
                        scatter(c)
                if before:
                    project(before)

            with pe.Fori(0, passes) as m:
                paired(m, pe, step1)

            all_groups(pe, lambda k: transpose_agg(k, k.it + NG // 2, (fin_even, fin_relu)))

    return nc


def kernel(x, src, dst, edge_attr_64, edge_type_8, edge_weight1, L0_gnn_We1, L0_gnn_be1, L0_gnn_We2, L0_gnn_be2,
           L0_gnn_Wn1, L0_gnn_bn1, L0_gnn_Wn2, L0_gnn_bn2, L1_gnn_W, L1_gnn_b):
    import numpy as np
    import concourse.bacc as bacc
    from concourse import mybir
    from concourse.bass_utils import run_bass_kernel_spmd

    nodes, width = x.shape
    edges = src.shape[0]
    group, chunk, tiles, block = 2 * 7 * 128, 512, 4, 2 * 512
    n_pad = -(-nodes // group) * group - nodes
    e_pad = -(-edges // block) * block - edges
    n_chunks = (edges + e_pad) // chunk

    def padded(a, n, value=0):
        a = np.asarray(a)
        return np.concatenate([a, np.full((n,) + a.shape[1:], value, a.dtype)])

    def by_partition(a):
        return np.ascontiguousarray(a.reshape(n_chunks, chunk // tiles, tiles).transpose(1, 0, 2).reshape(chunk // tiles, -1))

    def tile_major(a):
        return a.reshape(n_chunks, chunk // tiles, tiles).transpose(0, 2, 1).reshape(n_chunks, chunk)

    def edge_columns(a):
        a = a.reshape(n_chunks, chunk // tiles, 2, 2, a.shape[1])
        return a.transpose(0, 3, 4, 2, 1).reshape(n_chunks, 2 * a.shape[-1], 2 * chunk // tiles)

    dst_pad = padded(dst, e_pad, -1)
    arrays = {
        "x": padded(x, n_pad),
        "src_t": by_partition(padded(src, e_pad)),
        "dst_t": by_partition(dst_pad),
        "etype_t": by_partition(padded(edge_type_8, e_pad)),
        "weight_t": by_partition(padded(np.asarray(edge_weight1)[:, 0], e_pad)),
        "dst_c": padded(tile_major(dst_pad), -n_chunks % 16, -1),
        "edge_cols": edge_columns(padded(edge_attr_64, e_pad)),
        "we1": L0_gnn_We1, "be1": L0_gnn_be1, "we2": L0_gnn_We2, "be2": L0_gnn_be2,
        "wn1": L0_gnn_Wn1, "bn1": L0_gnn_bn1, "wn2": L0_gnn_Wn2, "bn2": L0_gnn_bn2,
        "w_rel": L1_gnn_W, "b_rel": L1_gnn_b,
    }
    arrays = {f"in_{k}": np.ascontiguousarray(a) for k, a in arrays.items()}
    nc = bacc.Bacc("TRN2", target_bir_lowering=False, num_devices=1)
    args = [nc.dram_tensor(k, a.shape, mybir.dt.from_np(a.dtype), kind="ExternalInput").ap() for k, a in arrays.items()]
    args.append(nc.dram_tensor("out_x", [nodes + n_pad, width], mybir.dt.float32, kind="ExternalOutput").ap())
    gnn_two_layers(nc, *args)
    got = run_bass_kernel_spmd(nc, [arrays], core_ids=[0])
    return got.results[0]["out_x"][:nodes]
```
